# Optimizing a Trainium2 kernel written in Bass

```python
import numpy as np
import jax
import jax.numpy as jnp

def _softmax(x, axis=-1):
    return jax.nn.softmax(x, axis=axis)

def _gelu(x):
    return jax.nn.gelu(x, approximate=True)

def _silu(x):
    return jax.nn.silu(x)

def _sigmoid(x):
    return jax.nn.sigmoid(x)

def _layernorm(x, axis=-1, eps=1e-05):
    m = jnp.mean(x, axis=axis, keepdims=True)
    v = jnp.var(x, axis=axis, keepdims=True)
    return (x - m) / jnp.sqrt(v + eps)

def _scatter_add(tgt, idx, src, axis=0):
    return tgt.at[idx].add(src)

def _segment_sum(src, seg, n):
    return jax.ops.segment_sum(src, seg, n)
kernel_name = 'mk_vit_tower_d1_tok_img768_r4_f00210'

def setup_inputs(seed: int=0):
    np.random.seed(seed)
    _w = jnp.asarray

    def _rec_inputs():
        import jax
        import jax.numpy as jnp
        _rk = jax.random.key(seed)
        x = -0.000596345 + 1.00056 * jax.random.normal(jax.random.fold_in(_rk, 1), (16, 3, 64, 64), jnp.float32)
        return x
    x = _rec_inputs()

    def _L0_tok_setup():
        import jax, jax.numpy as jnp
        import numpy as np
        B = 16
        IMG = 64
        CH = 3
        EMBED = 64
        GP = 16
        PRE = [1, 2, 4]
        N_LEVELS = 3
        FUSED = EMBED * N_LEVELS

        def hilbert_flat_indices(n):
            t = np.arange(n * n, dtype=np.int64)
            x = np.zeros(n * n, dtype=np.int64)
            y = np.zeros(n * n, dtype=np.int64)
            s = 1
            while s < n:
                rx = 1 & t // 2
                ry = 1 & (t ^ rx)
                swap = ry == 0
                flip = swap & (rx == 1)
                x = np.where(flip, s - 1 - x, x)
                y = np.where(flip, s - 1 - y, y)
                x2 = np.where(swap, y, x)
                y2 = np.where(swap, x, y)
                x, y = (x2, y2)
                x = x + s * rx
                y = y + s * ry
                t = t // 4
                s *= 2
            return y * n + x

        def _level(x, idx, W, b, p, gp):
            Bsz, C, H, _ = x.shape
            h = H // p
            t = x.reshape(Bsz, C, h, p, h, p).transpose(0, 2, 4, 3, 5, 1).reshape(Bsz, h * h, p * p * C)
            t = t[:, idx]
            t = t.reshape(Bsz, h * h // gp, gp * p * p * C)
            return t @ W.T + b

        def _interp_linear(x, n_out):
            L = x.shape[1]
            pos = (jnp.arange(n_out, dtype=jnp.float32) + 0.5) * (L / n_out) - 0.5
            pos = jnp.clip(pos, 0.0, L - 1)
            i0 = jnp.floor(pos).astype(jnp.int32)
            i1 = jnp.minimum(i0 + 1, L - 1)
            w = (pos - i0).astype(x.dtype)
            return x[:, i0] * (1.0 - w)[None, :, None] + x[:, i1] * w[None, :, None]
        key = jax.random.key(seed)
        ks = jax.random.split(key, 9)
        inp = {'x': jax.random.normal(ks[0], (B, CH, IMG, IMG), jnp.float32)}
        for i, p in enumerate(PRE):
            din = CH * p * p * GP
            inp[f'W{i}'] = jax.random.normal(ks[1 + 2 * i], (EMBED, din), jnp.float32) * din ** (-0.5)
            inp[f'b{i}'] = jax.random.normal(ks[2 + 2 * i], (EMBED,), jnp.float32) * 0.02
        inp['Wf'] = jax.random.normal(ks[7], (FUSED, FUSED), jnp.float32) * FUSED ** (-0.5)
        inp['bf'] = jax.random.normal(ks[8], (FUSED,), jnp.float32) * 0.02
        for i, p in enumerate(PRE):
            inp[f'idx{i}'] = jnp.asarray(hilbert_flat_indices(IMG // p), jnp.int32)
        return inp
    _L0_tok_all = _L0_tok_setup()
    _L0_tok_in = {k: v for k, v in _L0_tok_all.items() if k in ('W0', 'b0', 'W1', 'b1', 'W2', 'b2', 'Wf', 'bf', 'idx0', 'idx1', 'idx2')}
    del _L0_tok_all

    def _L0_attn_setup():
        import jax, jax.numpy as jnp
        import numpy as np
        B, S, D, H = (8, 256, 192, 12)
        HS = D // H
        key = jax.random.key(seed)
        k1, k2, k3 = jax.random.split(key, 3)
        x = jax.random.normal(k1, (B, S, D), dtype=jnp.float32)
        W_attn = jax.random.normal(k2, (D, 3 * H * HS), dtype=jnp.float32) * 0.02
        b_attn = jnp.zeros((3 * H * HS,), dtype=jnp.float32)
        W_proj = jax.random.normal(k3, (H * HS, D), dtype=jnp.float32) * 0.02
        b_proj = jnp.zeros((D,), dtype=jnp.float32)
        return {'x': x, 'W_attn': W_attn, 'b_attn': b_attn, 'W_proj': W_proj, 'b_proj': b_proj}
    _L0_attn_all = _L0_attn_setup()
    _L0_attn_in = {k: v for k, v in _L0_attn_all.items() if k in ('W_attn', 'b_attn', 'W_proj', 'b_proj')}
    del _L0_attn_all

    def _L0_ffn_setup():
        import jax, jax.numpy as jnp
        import numpy as np
        DEPTH = 11

        def _fff_forward(inputs, weights_in, weights_out, depth=DEPTH):
            B, S, _ = inputs.shape
            n_nodes = weights_in.shape[0]
            max_index = n_nodes - 1
            all_logits = jnp.einsum('bsd,nd->bsn', inputs, weights_in)

            def step(prev_idx, _):
                sel = jnp.clip(prev_idx, 0, max_index)
                logits = jnp.take_along_axis(all_logits, sel[..., None], axis=-1)[..., 0]
                new_idx = jnp.clip(2 * sel + 1 + (logits > 0).astype(sel.dtype), 0, max_index)
                return (new_idx, (logits, new_idx))
            idx0 = jnp.zeros((B, S), dtype=jnp.int32)
            _, (logits_seq, idx_seq) = jax.lax.scan(step, idx0, None, length=depth - 1)
            logits = jnp.concatenate([jnp.zeros((1, B, S), all_logits.dtype), logits_seq], axis=0)
            node_idx = jnp.concatenate([idx0[None], idx_seq], axis=0)
            act = jax.nn.gelu(logits, approximate=False)
            onehot = jax.nn.one_hot(node_idx, n_nodes, dtype=act.dtype)
            coeff = jnp.einsum('dbs,dbsn->bsn', act, onehot)
            return jnp.einsum('bsn,nd->bsd', coeff, weights_out)
        key = jax.random.key(seed)
        k1, k2, k3 = jax.random.split(key, 3)
        B, S, D = (4, 1024, 192)
        n_nodes = 2 * DEPTH - 1
        return {'inputs': jax.random.normal(k1, (B, S, D), dtype=jnp.float32), 'weights_in': jax.random.normal(k2, (n_nodes, D), dtype=jnp.float32), 'weights_out': jax.random.normal(k3, (n_nodes, D), dtype=jnp.float32)}
    _L0_ffn_all = _L0_ffn_setup()
    _L0_ffn_in = {k: v for k, v in _L0_ffn_all.items() if k in ('weights_in', 'weights_out')}
    del _L0_ffn_all
    return {'x': x, 'L0_tok_W0': _L0_tok_in['W0'], 'L0_tok_b0': _L0_tok_in['b0'], 'L0_tok_W1': _L0_tok_in['W1'], 'L0_tok_b1': _L0_tok_in['b1'], 'L0_tok_W2': _L0_tok_in['W2'], 'L0_tok_b2': _L0_tok_in['b2'], 'L0_tok_Wf': _L0_tok_in['Wf'], 'L0_tok_bf': _L0_tok_in['bf'], 'L0_tok_idx0': _L0_tok_in['idx0'], 'L0_tok_idx1': _L0_tok_in['idx1'], 'L0_tok_idx2': _L0_tok_in['idx2'], 'L0_attn_W_attn': _L0_attn_in['W_attn'], 'L0_attn_b_attn': _L0_attn_in['b_attn'], 'L0_attn_W_proj': _L0_attn_in['W_proj'], 'L0_attn_b_proj': _L0_attn_in['b_proj'], 'L0_ffn_weights_in': _L0_ffn_in['weights_in'], 'L0_ffn_weights_out': _L0_ffn_in['weights_out']}

def reference(x, L0_tok_W0, L0_tok_b0, L0_tok_W1, L0_tok_b1, L0_tok_W2, L0_tok_b2, L0_tok_Wf, L0_tok_bf, L0_tok_idx0, L0_tok_idx1, L0_tok_idx2, L0_attn_W_attn, L0_attn_b_attn, L0_attn_W_proj, L0_attn_b_proj, L0_ffn_weights_in, L0_ffn_weights_out):
    import jax
    import jax.numpy as jnp

    def _L0_tok_ref(x, W0, b0, W1, b1, W2, b2, Wf, bf, idx0, idx1, idx2):
        import jax, jax.numpy as jnp
        import numpy as np
        B = 16
        IMG = 64
        CH = 3
        EMBED = 64
        GP = 16
        PRE = [1, 2, 4]
        N_LEVELS = 3
        FUSED = EMBED * N_LEVELS

        def hilbert_flat_indices(n):
            t = np.arange(n * n, dtype=np.int64)
            x = np.zeros(n * n, dtype=np.int64)
            y = np.zeros(n * n, dtype=np.int64)
            s = 1
            while s < n:
                rx = 1 & t // 2
                ry = 1 & (t ^ rx)
                swap = ry == 0
                flip = swap & (rx == 1)
                x = np.where(flip, s - 1 - x, x)
                y = np.where(flip, s - 1 - y, y)
                x2 = np.where(swap, y, x)
                y2 = np.where(swap, x, y)
                x, y = (x2, y2)
                x = x + s * rx
                y = y + s * ry
                t = t // 4
                s *= 2
            return y * n + x

        def _level(x, idx, W, b, p, gp):
            Bsz, C, H, _ = x.shape
            h = H // p
            t = x.reshape(Bsz, C, h, p, h, p).transpose(0, 2, 4, 3, 5, 1).reshape(Bsz, h * h, p * p * C)
            t = t[:, idx]
            t = t.reshape(Bsz, h * h // gp, gp * p * p * C)
            return t @ W.T + b

        def _interp_linear(x, n_out):
            L = x.shape[1]
            pos = (jnp.arange(n_out, dtype=jnp.float32) + 0.5) * (L / n_out) - 0.5
            pos = jnp.clip(pos, 0.0, L - 1)
            i0 = jnp.floor(pos).astype(jnp.int32)
            i1 = jnp.minimum(i0 + 1, L - 1)
            w = (pos - i0).astype(x.dtype)
            return x[:, i0] * (1.0 - w)[None, :, None] + x[:, i1] * w[None, :, None]
        Ws = [(idx0, W0, b0, PRE[0]), (idx1, W1, b1, PRE[1]), (idx2, W2, b2, PRE[2])]
        outs = [_level(x, idx, W, b, p, GP) for idx, W, b, p in Ws]
        n_tokens = outs[0].shape[1]
        outs = [outs[0]] + [_interp_linear(o, n_tokens) for o in outs[1:]]
        y = jnp.concatenate(outs, axis=-1)
        return y @ Wf.T + bf

    def _L0_attn_ref(x, W_attn, b_attn, W_proj, b_proj):
        import jax, jax.numpy as jnp
        import numpy as np
        B, S, D, H = (8, 256, 192, 12)
        HS = D // H
        b, s, d = x.shape
        qkv = (x @ W_attn + b_attn).reshape(b, s, 3, H, HS)
        q, k, v = (qkv[:, :, 0], qkv[:, :, 1], qkv[:, :, 2])
        scale = jnp.sqrt(jnp.asarray(HS, dtype=x.dtype))
        scores = jnp.einsum('bqhd,bkhd->bhqk', q, k) / scale
        causal = jnp.tril(jnp.ones((s, s), dtype=bool))
        scores = jnp.where(causal, scores, -jnp.inf)
        attn = jax.nn.softmax(scores, axis=-1)
        out = jnp.einsum('bhqk,bkhd->bqhd', attn, v).reshape(b, s, H * HS)
        return out @ W_proj + b_proj

    def _L0_ffn_ref(inputs, weights_in, weights_out):
        import jax, jax.numpy as jnp
        import numpy as np
        DEPTH = 11

        def _fff_forward(inputs, weights_in, weights_out, depth=DEPTH):
            B, S, _ = inputs.shape
            n_nodes = weights_in.shape[0]
            max_index = n_nodes - 1
            all_logits = jnp.einsum('bsd,nd->bsn', inputs, weights_in)

            def step(prev_idx, _):
                sel = jnp.clip(prev_idx, 0, max_index)
                logits = jnp.take_along_axis(all_logits, sel[..., None], axis=-1)[..., 0]
                new_idx = jnp.clip(2 * sel + 1 + (logits > 0).astype(sel.dtype), 0, max_index)
                return (new_idx, (logits, new_idx))
            idx0 = jnp.zeros((B, S), dtype=jnp.int32)
            _, (logits_seq, idx_seq) = jax.lax.scan(step, idx0, None, length=depth - 1)
            logits = jnp.concatenate([jnp.zeros((1, B, S), all_logits.dtype), logits_seq], axis=0)
            node_idx = jnp.concatenate([idx0[None], idx_seq], axis=0)
            act = jax.nn.gelu(logits, approximate=False)
            onehot = jax.nn.one_hot(node_idx, n_nodes, dtype=act.dtype)
            coeff = jnp.einsum('dbs,dbsn->bsn', act, onehot)
            return jnp.einsum('bsn,nd->bsd', coeff, weights_out)
        return _fff_forward(inputs, weights_in, weights_out)
    h = _L0_tok_ref(x, L0_tok_W0, L0_tok_b0, L0_tok_W1, L0_tok_b1, L0_tok_W2, L0_tok_b2, L0_tok_Wf, L0_tok_bf, L0_tok_idx0, L0_tok_idx1, L0_tok_idx2)
    h = h + _L0_attn_ref(_layernorm(h, axis=-1), L0_attn_W_attn, L0_attn_b_attn, L0_attn_W_proj, L0_attn_b_proj)
    h = h + _L0_ffn_ref(_layernorm(h, axis=-1), L0_ffn_weights_in, L0_ffn_weights_out)
    return h

_drawn_inputs = setup_inputs


def setup_inputs(seed=0):
    import zlib

    import numpy as np

    out = dict(_drawn_inputs(seed))
    spreads = {'L0_attn_b_attn': (0.0, 0.1), 'L0_attn_b_proj': (0.0, 0.1)}
    factors = {}
    for name, (base, spread) in spreads.items():
        noise = np.random.default_rng([zlib.crc32(name.encode()), seed]).standard_normal(out[name].shape)
        drawn = base * np.exp(spread * noise) if base else spread * noise
        out[name] = jnp.asarray(drawn.astype(out[name].dtype))
    for name, factor in factors.items():
        out[name] = (out[name] * factor).astype(out[name].dtype)
    return out
```

```python
import concourse.bass as bass
from concourse import mybir
from contextlib import ExitStack

B, CH, IMG = 16, 3, 64
GP, EMB = 16, 64
D = 3 * EMB
S = IMG * IMG // GP
P = 128
TT = S // P
NT = B * TT
H, HS = 12, 16
HALF = D // 2
F0, F1, F2 = CH, 4 * CH, 16 * CH
T1, T2 = S // 4, S // 16
NODES = 21
NCO = 32
EPS = 1e-5
PARTS = 3
KQ = 6 * HS
NM = 2 * H
SU = 9
SCALE = 0.25


class Image:

    def __init__(self, pair, off):
        self.pair, self.off = pair, off
        number = off if isinstance(pair, int) else None
        self.first, self.second, self.last = number == 0, number == 1, number == B - 1

    def __add__(self, n):
        return Image(self.pair, self.off + n)

    def __sub__(self, n):
        return Image(self.pair, self.off - n)

    def count(self, per, more=0):
        return self.pair * (2 * per) + (self.off * per + more)


def vit_tower_kernel(nc, x0, x1, x2, ix0, ix1, ix2, w0, w1t, w2t, wft, bcol, bf,
                     wa, bqk, bv, wp, bp, wint, wext, identf, identb, maskq, maskk, sel, interp,
                     out, parts):
    fp32, bf16, i32 = mybir.dt.float32, mybir.dt.bfloat16, mybir.dt.int32
    ALU = mybir.AluOpType
    ACT = mybir.ActivationFunctionType
    AX = mybir.AxisListType

    ctx = ExitStack()
    with ctx:
        def sb(name, shape, dt=fp32):
            return ctx.enter_context(nc.sbuf_tensor(name, shape, dt))

        def sem(name):
            return ctx.enter_context(nc.semaphore(name))

        ID = sb("ID", [P, P])
        IDB = sb("IDB", [P, P], bf16)
        MASKQ = sb("MASKQ", [P, 4, P], bf16)
        MASKK = sb("MASKK", [P, 4, P], bf16)
        SEL = sb("SEL", [NM, H, P], bf16)
        W0S = sb("W0S", [EMB, GP * F0])
        W1S = sb("W1S", [HALF, 2, EMB])
        W2S = sb("W2S", [F2, GP, EMB])
        WFS = sb("WFS", [EMB, 3, D])
        WA = sb("WA", [HALF, 2, 3 * D])
        WP = sb("WP", [HALF, 2, D])
        WIN = sb("WIN", [HALF, 2, NODES])
        WEX = sb("WEX", [NCO, D])
        BC = sb("BC", [EMB, 3])
        BFB = sb("BFB", [P, D])
        BQK = sb("BQK", [HALF, 4])
        BV = sb("BV", [P, D])
        BP = sb("BP", [P, D])

        I0 = sb("I0", [P, TT * GP], i32)
        I1 = sb("I1", [P, GP // 2], i32)
        I2 = sb("I2", [P, 2], i32)
        CB = sb("CB", [P, D])
        C0 = sb("C0", [GP * F0, D])
        HT = sb("HT", [P, NT, D])
        ST = sb("ST", [P, NT, 6])
        MV = sb("MV", [P, NT, 2])
        VE = sb("VE", [P, NT])
        SD = sb("SD", [P, NT])
        RSTD = sb("RSTD", [P, NT])
        NMR = sb("NMR", [P, NT])

        XN = sb("XN", [P, TT, D])
        XNT = sb("XNT", [HALF, 2, S])
        PART = [sb(f"PART{i}", [HALF, 4, S], bf16) for i in range(PARTS)]
        RES = sb("RES", [HALF, 4, S])
        VA = [sb(f"VA{i}", [P, TT, H, 32]) for i in range(2)]
        MX = sb("MX", [P, TT, H])
        MP = sb("MP", [P, TT, 2, H], bf16)
        MT = sb("MT", [NM, S], bf16)
        OT = sb("OT", [P, 3, S])
        RC = sb("RC", [P, TT, H])
        ON = sb("ON", [P, TT, D])
        ONT = sb("ONT", [HALF, 2, S])
        H2 = sb("H2", [P, TT, D])
        MV2 = sb("MV2", [P, TT, 2])
        ST2 = sb("ST2", [P, TT, 6])

        CO = sb("CO", [P, NT, NCO])
        with ExitStack() as early:
            tok = lambda name, shape, dt=fp32: early.enter_context(nc.sbuf_tensor(name, shape, dt))
            G0 = tok("G0", [P, TT, GP, B * F0])
            G1 = tok("G1", [P, GP // 2, B * F1])
            G2 = tok("G2", [P, 2, B * F2])
            G0R = tok("G0R", [P, TT, B, GP * F0])
            G1R = tok("G1R", [P, B, HALF])
            G1T = tok("G1T", [HALF, 2, B, T1])
            G2T = tok("G2T", [F2, GP, B, T2])
            E1 = tok("E1", [EMB, B * T1])
            E2 = tok("E2", [EMB, B * T2])
            Z2 = tok("Z2", [P, 2, D])
            LH = tok("LH", [P, NT, P])
            RH = tok("RH", [P, B, D])

        QS = [sb(f"QS{i}", [KQ, H, S], bf16) for i in range(2)]
        KS = [sb(f"KS{i}", [KQ, H, S], bf16) for i in range(2)]
        PT = sb("PT", [P, SU, 512])

        X2 = sb("X2", [P, 4, D])
        X2T = [sb(f"X2T{i}", [HALF, 2, P]) for i in range(4)]
        LG = sb("LG", [P, NT, NODES])
        GE = sb("GE", [P, NT, NODES])
        SG = sb("SG", [P, NT, NODES])
        NS = sb("NS", [P, NT, NODES])
        RE = sb("RE", [P, NT, 22])
        QQ = sb("QQ", [P, NT, 10])
        COT = [sb(f"COT{i}", [NCO, P]) for i in range(4)]
        OUTS = sb("OUTS", [P, 4, 2 * D])

        BANK = [ctx.enter_context(nc.psum_tensor(f"bank{i}", [P, 512], fp32)) for i in range(8)]

        ld_idx, ld_const, ld_interp, ld_z2 = sem("ld_idx"), sem("ld_const"), sem("ld_interp"), sem("ld_z2")
        g2_in, g1_in = sem("g2_in"), sem("g1_in")
        g1r_ok, g0r_ok = sem("g1r_ok"), sem("g0r_ok")
        g0_in = [sem(f"g0_in{t}") for t in range(TT)]
        pe_a, pe_d = sem("pe_a"), sem("pe_d")
        act_a, dve_d = sem("act_a"), sem("dve_d")
        va_init = sem("va_init")
        stat, var_ok, sd_ok, rstd_ok, nmr_ok = sem("stat"), sem("var_ok"), sem("sd_ok"), sem("rstd_ok"), sem("nmr_ok")
        xn_ok, xt_ps, xnt_ok, qk_ps, p0_ok, r_ok, p1_ok, p2_ok = [
            sem(n) for n in ("xn_ok", "xt_ps", "xnt_ok", "qk_ps", "p0_ok", "r_ok", "p1_ok", "p2_ok")]
        stored, stacked = sem("stored"), sem("stacked")
        v_ps, v_ok = sem("v_ps"), sem("v_ok")
        s_ps, max_ok, mh_ok, mp_ok, mt_ps, mt_ok = [
            sem(n) for n in ("s_ps", "max_ok", "mh_ok", "mp_ok", "mt_ps", "mt_ok")]
        st_ps, exp_ok, av_ps, ot_ok = sem("st_ps"), sem("exp_ok"), sem("av_ps"), sem("ot_ok")
        t1_ps, rc_ok, on_ok, t2_ps, ont_ok, pj_ps, h2_ok = [
            sem(n) for n in ("t1_ps", "rc_ok", "on_ok", "t2_ps", "ont_ok", "pj_ps", "h2_ok")]
        st2_ok, mv2_ok, mvh_ok = sem("st2_ok"), sem("mv2_ok"), sem("mvh_ok")
        x2_ok, x2t_ps, x2t_ok, lg_ps, lg_ok, ge_ok, tree = [
            sem(n) for n in ("x2_ok", "x2t_ps", "x2t_ok", "lg_ps", "lg_ok", "ge_ok", "tree")]
        co_ok, cot_ps, cot_ok, o_ps, o_ok = [
            sem(n) for n in ("co_ok", "cot_ps", "cot_ok", "o_ps", "o_ok")]
        out_ok = [sem(f"out_ok{n}") for n in range(2)]

        N_CONST = 18
        S_BANK = [0, 1]
        T_BANK = [2, 3]
        O_BANK = [4, 5]
        MA, MB = 6, 7

        block = ctx.enter_context(nc.Block())

        @block.sync
        def _(sp):
            for t, src in ((I2, ix2), (I1, ix1), (I0, ix0)):
                sp.dma_start(t[:, :], src).then_inc(ld_idx, 16)
            sp.dma_start(ID[:, :], identf).then_inc(ld_const, 16)
            sp.dma_start(W2S[:, :, :], w2t.rearrange("(g f) e -> f g e", g=GP)).then_inc(ld_const, 16)
            sp.dma_start(W1S[:, :, :], w1t.rearrange("(g f) e -> f g e", g=2)).then_inc(ld_const, 16)
            sp.dma_start(WFS[:, :, :], wft.rearrange("(l e) o -> e l o", l=3)).then_inc(ld_const, 16)
            sp.dma_start(W0S[:, :], w0).then_inc(ld_const, 16)
            sp.dma_start(BC[:, :], bcol).then_inc(ld_const, 16)
            for t, src in ((BFB, bf), (BV, bv), (BP, bp)):
                sp.dma_start(t[:, :], src.rearrange("(a n) -> a n", a=1).broadcast_to([P, D])).then_inc(ld_const, 16)
            sp.dma_start(LH[GP * F0:P, :, :].rearrange("k (b t) n -> k b (t n)", b=B),
                         interp.rearrange("k (a n) -> k a n", a=1).broadcast_to([T2 + T1, B, S])).then_inc(ld_interp, 16)
            sp.dma_start(BQK[:, :], bqk).then_inc(ld_const, 16)
            sp.dma_start(WA[:, :, :], wa.rearrange("(k p) n -> p k n", k=2)).then_inc(ld_const, 16)
            sp.dma_start(WP[:, :, :], wp.rearrange("(k p) n -> p k n", k=2)).then_inc(ld_const, 16)
            sp.dma_start(WIN[:, :, :], wint.rearrange("(k p) n -> p k n", k=2)).then_inc(ld_const, 16)
            sp.dma_start(WEX[:, :], wext).then_inc(ld_const, 16)
            sp.dma_start(IDB[:, :], identb).then_inc(ld_const, 16)
            sp.dma_start(MASKQ[:, :, :], maskq.rearrange("q (a k) -> q a k", a=1).broadcast_to([P, 4, P])).then_inc(ld_const, 16)
            sp.dma_start(MASKK[:, :, :], maskk.rearrange("q (a k) -> q a k", a=1).broadcast_to([P, 4, P])).then_inc(ld_const, 16)
            sp.dma_start(SEL[:, :, :], sel).then_inc(ld_const, 16)
            sp.wait_ge(act_a, 18)
            for b in range(B):
                r = (b % 8) * T2
                sp.dma_start(RH[GP * F0:GP * F0 + T2, b, :], Z2[r:r + T2, b // 8, :]).then_inc(ld_z2, 16)

            def restack(b, par):
                def fixed(value):
                    return value if isinstance(value, int) else sp.snap(value)

                image, part0, part12 = fixed(b.count(1)), fixed(b.count(2, 2)), fixed(b.count(1, 1))
                in_dram = fixed(b.count(16 * PARTS, 16 * PARTS))
                for n, (ready, value) in enumerate(((p0_ok, part0), (p1_ok, part12), (p2_ok, part12))):
                    sp.wait_ge(ready, value)
                    sp.dma_start(parts[bass.ds(image, 1), n, :, :, :].rearrange("a m p s -> p (a m) s"),
                                 PART[n][:, :, :]).then_inc(stored, 16)
                sp.wait_ge(stored, in_dram)
                view = parts[bass.ds(image, 1), :, :, :, :].rearrange("a n (w m) p s -> (a n) w (m p) s", w=2)
                for r, (pq, pk) in enumerate(((0, 0), (0, 1), (0, 2), (1, 0), (1, 1), (2, 0))):
                    for dst, w, n in ((QS[par], 0, pq), (KS[par], 1, pk)):
                        sp.dma_start(dst[r * HS:(r + 1) * HS, :, :],
                                     view[n, w, :, :].rearrange("(h d) s -> d h s", h=H)).then_inc(stacked, 16)

            for par in range(2):
                restack(Image(0, par), par)
            with sp.Fori(0, (B - 2) // 2) as i:
                for par in range(2):
                    restack(Image(i, 2 + par), par)

            for k in range(NT // 4):
                sp.wait_ge(o_ok, 2 * k + 2)
                sp.dma_start(out[4 * k * P:(4 * k + 4) * P, :].rearrange("(t p) d -> p t d", p=P),
                             OUTS[:, 2 * (k % 2):2 * (k % 2) + 2, :].rearrange("p a (t d) -> p (a t) d", d=D)).then_inc(out_ok[k % 2], 16)
            for n in range(2):
                sp.wait_ge(out_ok[n], 16 * (NT // 8))

        @block.gpsimd
        def _(pool):
            pool.wait_ge(ld_idx, 48)
            for j in range(2):
                pool.indirect_dma_start(G2[:, j, :], None, x2, bass.IndirectOffsetOnAxis(ap=I2[:, j:j + 1], axis=0)).then_inc(g2_in, 16)
            for j in range(GP // 2):
                pool.indirect_dma_start(G1[:, j, :], None, x1, bass.IndirectOffsetOnAxis(ap=I1[:, j:j + 1], axis=0)).then_inc(g1_in, 16)
            for t in range(TT):
                for g in range(GP):
                    j = t * GP + g
                    pool.indirect_dma_start(G0[:, t, g, :], None, x0, bass.IndirectOffsetOnAxis(ap=I0[:, j:j + 1], axis=0)).then_inc(g0_in[t], 16)
            for i in range(2):
                pool.memset(VA[i][:, :, :, HS:32], 0.0).then_inc(va_init, 1)
            pool.wait_ge(va_init, 2)
            for i in range(2):
                pool.memset(VA[i][:, :, :, HS:HS + 1], 1.0).then_inc(va_init, 1)
            pool.memset(CO[:, :, 0:1], 0.0).then_inc(va_init, 1)

            def low(b):
                pool.wait_ge(p1_ok, b.count(1, 1))
                pool.tensor_tensor(PART[2][:, :, :], RES[:, :, :], PART[1][:, :, :], ALU.subtract).then_inc(p2_ok, 1)

            low(Image(0, 0))
            with pool.Fori(0, B // 2 - 1) as i:
                for par in range(2):
                    low(Image(i, 1 + par))
            low(Image(0, B - 1))

        @block.scalar
        def _(act):
            act.wait_ge(ld_const, 16 * N_CONST)
            job = 0

            def a_bank():
                return BANK[job % 4]

            for b in range(B):
                act.wait_ge(pe_a, job + 1)
                nc.scalar.copy(G2T[:, :, b, :], a_bank()[0:F2, 0:2 * P].rearrange("f (g t) -> f g t", t=T2)).then_inc(act_a, 1)
                job += 1
            act.wait_ge(pe_a, job + 1)
            nc.scalar.activation(E2[:, :], a_bank()[0:EMB, 0:B * T2], ACT.Identity, bias=BC[:, 2:3]).then_inc(act_a, 1)
            job += 1
            act.wait_ge(pe_a, job + 1)
            nc.scalar.copy(Z2[:, :, :], a_bank()[:, 0:2 * D].rearrange("p (a d) -> p a d", a=2)).then_inc(act_a, 1)
            job += 1
            for c in range(2):
                act.wait_ge(pe_a, job + 1)
                nc.scalar.activation(E1[:, c * 512:(c + 1) * 512], a_bank()[0:EMB, :], ACT.Identity, bias=BC[:, 1:2]).then_inc(act_a, 1)
                job += 1
            act.wait_ge(dve_d, 6)
            nc.scalar.copy(RH[0:GP * F0, :, :], C0[:, :].rearrange("p (a d) -> p a d", a=1).broadcast_to([GP * F0, B, D])).then_inc(act_a, 1)
            act_extra = 1
            for t in range(TT):
                for q in range(4):
                    act.wait_ge(pe_a, job + 1)
                    nc.scalar.copy(LH[0:GP * F0, :, :].rearrange("k (b t) n -> k b t n", t=TT)[:, 4 * q:4 * q + 4, t, :],
                                   a_bank()[0:GP * F0, :].rearrange("k (b n) -> k b n", b=4)).then_inc(act_a, 1)
                    job += 1
            act.wait_ge(var_ok, 1)
            nc.scalar.activation(SD[:, :], VE[:, :], ACT.Sqrt).then_inc(sd_ok, 1)

            def front(b):
                act.wait_ge(xt_ps, b.count(1, 1))
                nc.scalar.copy(XNT[:, :, :], BANK[MB][0:HALF, :].rearrange("p (k s) -> p k s", k=2)).then_inc(xnt_ok, 1)

            def first_part(b, w):
                act.wait_ge(qk_ps, b.count(2, w + 1))
                if w == 0 and not b.first:
                    act.wait_ge(stored, b.count(16 * PARTS))
                for m in range(2):
                    ins = nc.scalar.activation(PART[0][:, 2 * w + m, :], BANK[MB][0:HALF, m * S:(m + 1) * S],
                                               ACT.Identity, bias=BQK[:, 2 * w + m:2 * w + m + 1])
                ins.then_inc(p0_ok, 1)

            def outputs_t(b):
                act.wait_ge(t2_ps, b.count(1, 1))
                nc.scalar.copy(ONT[:, :, :], BANK[MA][0:HALF, :].rearrange("p (k s) -> p k s", k=2)).then_inc(ont_ok, 1)

            def out_group(b, late):
                if late:
                    act.wait_ge(av_ps, b.count(3, 3))
                    nc.scalar.copy(OT[:, 2, :], BANK[O_BANK[1]][:, 0:S]).then_inc(ot_ok, 1)
                else:
                    act.wait_ge(av_ps, b.count(3, 2))
                    nc.scalar.copy(OT[:, 0:2, :], BANK[O_BANK[0]][:, :].rearrange("p (g s) -> p g s", g=2)).then_inc(ot_ok, 1)

            def step(b, par, has_front, has_back):
                if has_back:
                    out_group(b - 1, True)
                if has_front:
                    front(b + 1)
                    first_part(b + 1, 0)
                    first_part(b + 1, 1)
                if has_back:
                    outputs_t(b - 1)
                act.wait_ge(mt_ps, b.count(1, 1))
                nc.scalar.copy(MT[:, :], BANK[MB][0:NM, 0:S // 2].bitcast(bf16)).then_inc(mt_ok, 1)
                for v in range(SU):
                    act.wait_ge(st_ps, b.count(SU, v + 1))
                    if has_back and v % 3 == 0:
                        act.wait_ge(av_ps, (b - 1).count(3, v // 3 + 1))
                    nc.scalar.activation(PT[:, v, :], BANK[T_BANK[(SU * par + v) % 2]][:, :], ACT.Exp, scale=SCALE).then_inc(exp_ok, 1)
                if has_back:
                    act.wait_ge(t1_ps, b.count(2))
                out_group(b, False)

            front(Image(0, 0))
            first_part(Image(0, 0), 0)
            first_part(Image(0, 0), 1)
            step(Image(0, 0), 0, True, False)
            with act.Fori(0, (B - 2) // 2) as i:
                step(Image(i, 1), 1, True, True)
                step(Image(i, 2), 0, True, True)
            step(Image(0, B - 1), 1, False, True)
            out_group(Image(0, B - 1), True)
            outputs_t(Image(0, B - 1))

            act.wait_ge(var_ok, 2)
            nc.scalar.activation(SD[:, :], VE[:, :], ACT.Sqrt).then_inc(sd_ok, 1)
            for k in range(NT):
                act.wait_ge(x2t_ps, k + 1)
                if k >= 4:
                    act.wait_ge(lg_ps, k - 3)
                nc.scalar.copy(X2T[k % 4][:, :, :], BANK[k % 2][0:HALF, 0:2 * P].rearrange("p (k s) -> p k s", k=2)).then_inc(x2t_ok, 1)
            act.wait_ge(lg_ok, NT // 8)
            nc.scalar.activation(GE[:, :, :], LG[:, :, :], ACT.Gelu).then_inc(ge_ok, 1)
            for k in range(NT):
                act.wait_ge(cot_ps, k + 1)
                if k >= 4:
                    act.wait_ge(o_ps, (k - 4) // 2 + 1)
                nc.scalar.copy(COT[k % 4][:, :], BANK[k % 2][0:NCO, 0:P]).then_inc(cot_ok, 1)

        @block.vector
        def _(dve):
            dve.wait_ge(ld_const, 16 * N_CONST)
            job = 0

            def d_bank():
                return BANK[4 + job % 4]

            dve.wait_ge(g1_in, 16 * (GP // 2))
            nc.vector.tensor_copy(G1R[:, :, :].rearrange("p b (g f) -> p g b f", f=F1), G1[:, :, :].rearrange("p g (b f) -> p g b f", f=F1)).then_inc(g1r_ok, 1)
            for q in range(4):
                dve.wait_ge(pe_d, job + 1)
                nc.vector.tensor_copy(G1T[:, :, 4 * q:4 * q + 4, :],
                                      d_bank()[0:HALF, :].rearrange("p (b g t) -> p g b t", b=4, g=2)).then_inc(dve_d, 1)
                job += 1
            dve.wait_ge(pe_d, job + 1)
            nc.vector.tensor_tensor(CB[:, :], d_bank()[:, 0:D], BFB[:, :], ALU.add).then_inc(dve_d, 1)
            job += 1
            dve.wait_ge(pe_d, job + 1)
            nc.vector.tensor_copy(C0[:, :], d_bank()[0:GP * F0, 0:D]).then_inc(dve_d, 1)
            job += 1
            dve.wait_ge(dve_d, 6)
            for q in range(B // 2):
                dve.wait_ge(pe_d, job + 1)
                nc.vector.tensor_tensor(RH[T1:P, 2 * q:2 * q + 2, :], d_bank()[T1:P, 0:2 * D].rearrange("p (b d) -> p b d", b=2),
                                        CB[T1:P, :].rearrange("p (a d) -> p a d", a=1).broadcast_to([T1, 2, D]), ALU.add).then_inc(dve_d, 1)
                job += 1
            done = 0
            for t in range(TT):
                dve.wait_ge(g0_in[t], 16 * GP)
                nc.vector.tensor_copy(G0R[:, t, :, :].rearrange("p b (g f) -> p g b f", f=F0),
                                      G0[:, t, :, :].rearrange("p g (b f) -> p g b f", f=F0)).then_inc(g0r_ok, 1)
                for q in range(B // 2):
                    dve.wait_ge(pe_d, job + 1)
                    view = HT[:, :, :].rearrange("p (b t) d -> p b t d", t=TT)[:, 2 * q:2 * q + 2, t, :]
                    nc.vector.tensor_copy(view, d_bank()[:, 0:2 * D].rearrange("p (b d) -> p b d", b=2)).then_inc(dve_d, 1)
                    job += 1
                    dve.wait_ge(dve_d, job)
                    for b in (2 * q, 2 * q + 1):
                        nc.vector.bn_stats(ST[:, TT * b + t, :], HT[:, TT * b + t, :]).then_inc(stat, 1)
                        done += 1
            dve.wait_ge(stat, NT)
            for k in range(NT):
                nc.vector.bn_aggr(MV[:, k, :], ST[:, k, :]).then_inc(stat, 1)

            def rstd(round_):
                nc.vector.tensor_scalar(VE[:, :], MV[:, :, 1], EPS, None, ALU.add).then_inc(var_ok, 1)
                dve.wait_ge(sd_ok, round_)
                nc.vector.reciprocal(RSTD[:, :], SD[:, :]).then_inc(rstd_ok, 1)
                dve.wait_ge(rstd_ok, round_)
                nc.vector.scalar_tensor_tensor(NMR[:, :], MV[:, :, 0], -1.0, RSTD[:, :], ALU.mult, ALU.mult).then_inc(nmr_ok, 1)

            dve.wait_ge(stat, 2 * NT)
            rstd(1)
            dve.wait_ge(va_init, 4)

            def norm(b):
                if not b.first:
                    dve.wait_ge(xt_ps, b.count(1))
                for t in range(TT):
                    k = b.count(TT, t)
                    ins = nc.vector.tensor_scalar(XN[:, t, :], HT[:, bass.ds(k, 1), :].rearrange("p a d -> p (a d)"),
                                                  RSTD[:, bass.ds(k, 1)], NMR[:, bass.ds(k, 1)], ALU.mult, ALU.add)
                ins.then_inc(xn_ok, 1)

            def row_max(b, par, u):
                dve.wait_ge(s_ps, b.count(SU, u + 1))
                if u == 0 and not b.first:
                    dve.wait_ge(mp_ok, b.count(1))
                bank = BANK[S_BANK[(SU * par + u) % 2]]
                if u < 3:
                    nc.vector.reduce_max(MX[:, 0, 4 * u:4 * u + 4], bank[:, :].rearrange("p (h k) -> p h k", h=4), AX.X).then_inc(max_ok, 1)
                else:
                    nc.vector.reduce_max(MX[:, 1, 2 * (u - 3):2 * (u - 3) + 2], bank[:, :].rearrange("p (h k) -> p h k", h=2), AX.X).then_inc(max_ok, 1)

            def rest(b, w):
                dve.wait_ge(p0_ok, b.count(2, w + 1))
                if w == 0 and not b.first:
                    dve.wait_ge(p2_ok, b.count(1))
                for m in range(2):
                    ins = nc.vector.scalar_tensor_tensor(RES[:, 2 * w + m, :], BANK[MB][0:HALF, m * S:(m + 1) * S],
                                                         BQK[:, 2 * w + m:2 * w + m + 1], PART[0][:, 2 * w + m, :], ALU.add, ALU.subtract)
                ins.then_inc(r_ok, 1)

            def middle(b):
                dve.wait_ge(r_ok, b.count(2, 2))
                nc.vector.tensor_copy(PART[1][:, :, :], RES[:, :, :]).then_inc(p1_ok, 1)

            def values(b, par):
                dve.wait_ge(v_ps, b.count(1, 1))
                if not (b.first or b.second):
                    dve.wait_ge(av_ps, (b - 1).count(3))
                for t in range(TT):
                    ins = nc.vector.tensor_tensor(VA[par][:, t, :, 0:HS], BANK[MB][:, t * D:(t + 1) * D].rearrange("p (h d) -> p h d", h=H),
                                                  BV[:, :].rearrange("p (h d) -> p h d", h=H), ALU.add)
                ins.then_inc(v_ok, 1)

            def normalise(b, t):
                dve.wait_ge(t1_ps, b.count(2, t + 1))
                o = BANK[MA][:, 0:3 * P].rearrange("p (h c) -> p h c", h=H)
                nc.vector.reciprocal(RC[:, t, :], o[:, :, HS]).then_inc(rc_ok, 1)
                dve.wait_ge(rc_ok, b.count(2, t + 1))
                nc.vector.tensor_tensor(ON[:, t, :].rearrange("p (h c) -> p h c", h=H), o[:, :, 0:HS],
                                        RC[:, t, :].rearrange("p (h a) -> p h a", a=1).broadcast_to([P, H, HS]), ALU.mult).then_inc(on_ok, 1)

            def minus_max(b):
                dve.wait_ge(max_ok, b.count(SU, SU))
                if not b.first:
                    dve.wait_ge(mt_ps, b.count(1))
                nc.vector.tensor_scalar(MP[:, :, 0, :], MX[:, :, :], -1.0, None, ALU.mult).then_inc(mh_ok, 1)
                dve.wait_ge(mh_ok, b.count(1, 1))
                nc.vector.scalar_tensor_tensor(MP[:, :, 1, :], MX[:, :, :], -1.0, MP[:, :, 0, :], ALU.mult, ALU.subtract).then_inc(mp_ok, 1)

            def residual(b):
                dve.wait_ge(pj_ps, b.count(1, 1))
                hv = HT[:, bass.ds(b.count(TT), TT), :]
                nc.vector.tensor_tensor(H2[:, :, :], BANK[MA][:, 0:2 * D].rearrange("p (t d) -> p t d", t=2), hv, ALU.add).then_inc(h2_ok, 1)
                dve.wait_ge(h2_ok, b.count(2, 1))
                nc.vector.tensor_tensor(H2[:, :, :], H2[:, :, :], BP[:, :].rearrange("p (a d) -> p a d", a=1).broadcast_to([P, 2, D]),
                                        ALU.add).then_inc(h2_ok, 1)
                dve.wait_ge(h2_ok, b.count(2, 2))
                for t in range(TT):
                    nc.vector.bn_stats(ST2[:, t, :], H2[:, t, :]).then_inc(st2_ok, 1)
                dve.wait_ge(st2_ok, b.count(2, 2))
                nc.vector.tensor_scalar(hv, H2[:, :, :], 1.0, None, ALU.mult)
                for t in range(TT):
                    nc.vector.bn_aggr(MV2[:, t, :], ST2[:, t, :]).then_inc(mv2_ok, 1)
                dve.wait_ge(mv2_ok, b.count(2, 2))
                nc.vector.tensor_scalar(MV[:, bass.ds(b.count(TT), TT), :], MV2[:, :, :], 1.0, None, ALU.mult).then_inc(mvh_ok, 1)

            def step(b, par, has_front, has_back):
                if has_front:
                    norm(b + 1)
                row_max(b, par, 0)
                row_max(b, par, 1)
                row_max(b, par, 2)
                if has_back:
                    normalise(b - 1, 0)
                row_max(b, par, 3)
                if has_front:
                    rest(b + 1, 0)
                row_max(b, par, 4)
                if has_back:
                    normalise(b - 1, 1)
                row_max(b, par, 5)
                if has_front:
                    rest(b + 1, 1)
                    middle(b + 1)
                row_max(b, par, 6)
                row_max(b, par, 7)
                row_max(b, par, 8)
                minus_max(b)
                if has_front:
                    values(b + 1, 1 - par)
                if has_back:
                    residual(b - 1)

            dve.wait_ge(nmr_ok, 1)
            norm(Image(0, 0))
            rest(Image(0, 0), 0)
            rest(Image(0, 0), 1)
            middle(Image(0, 0))
            values(Image(0, 0), 0)
            step(Image(0, 0), 0, True, False)
            with dve.Fori(0, (B - 2) // 2) as i:
                step(Image(i, 1), 1, True, True)
                step(Image(i, 2), 0, True, True)
            step(Image(0, B - 1), 1, False, True)
            normalise(Image(0, B - 1), 0)
            normalise(Image(0, B - 1), 1)
            residual(Image(0, B - 1))

            dve.wait_ge(mvh_ok, B)
            rstd(2)
            dve.wait_ge(nmr_ok, 2)
            for k in range(NT):
                if k >= 4:
                    dve.wait_ge(x2t_ps, k - 3)
                nc.vector.tensor_scalar(X2[:, k % 4, :], HT[:, k, :], RSTD[:, k:k + 1], NMR[:, k:k + 1], ALU.mult, ALU.add).then_inc(x2_ok, 1)
                if k % 8 == 7 and k > 8:
                    g = k // 8 - 1
                    dve.wait_ge(lg_ps, 8 * (g + 1))
                    nc.vector.tensor_copy(LG[:, 8 * g:8 * g + 8, :], BANK[4 + g % 2][:, 0:8 * NODES].rearrange("p (t n) -> p t n", t=8)).then_inc(lg_ok, 1)
            g = NT // 8 - 1
            dve.wait_ge(lg_ps, NT)
            nc.vector.tensor_copy(LG[:, 8 * g:8 * g + 8, :], BANK[4 + g % 2][:, 0:8 * NODES].rearrange("p (t n) -> p t n", t=8)).then_inc(lg_ok, 1)

            links = [0]

            def link(ins):
                links[0] += 1
                ins.then_inc(tree, 1)
                dve.wait_ge(tree, links[0])

            dve.wait_ge(lg_ok, NT // 8)
            nc.vector.tensor_scalar(SG[:, :, :], LG[:, :, :], 0.0, None, ALU.is_gt).then_inc(tree, 1)
            nc.vector.tensor_scalar(NS[:, :, :], LG[:, :, :], 0.0, None, ALU.is_le).then_inc(tree, 1)
            links[0] += 2
            link(nc.vector.memset(RE[:, :, 0:1], 1.0))
            for lo, hi in ((0, 1), (1, 3), (3, 7), (7, 10)):
                kids = RE[:, :, 2 * lo + 1:2 * hi + 1].rearrange("p t (n c) -> p t n c", c=2)
                nc.vector.tensor_tensor(kids[:, :, :, 0], RE[:, :, lo:hi], NS[:, :, lo:hi], ALU.mult).then_inc(tree, 1)
                links[0] += 1
                link(nc.vector.tensor_tensor(kids[:, :, :, 1], RE[:, :, lo:hi], SG[:, :, lo:hi], ALU.mult))
            link(nc.vector.reduce_sum(RE[:, :, 21:22].rearrange("p t a -> p (t a)"), RE[:, :, 15:20], AX.X))
            link(nc.vector.tensor_scalar(RE[:, :, 20:21], RE[:, :, 21:22], -1.0, 6.0, ALU.mult, ALU.add))
            dve.wait_ge(ge_ok, 1)
            nc.vector.tensor_tensor(CO[:, :, 21:32], RE[:, :, 10:21], GE[:, :, 10:21], ALU.mult).then_inc(tree, 1)
            links[0] += 1
            link(nc.vector.tensor_tensor(QQ[:, :, :], RE[:, :, 0:10], GE[:, :, 0:10], ALU.mult))
            kids = CO[:, :, 1:21].rearrange("p t (n c) -> p t n c", c=2)
            nc.vector.tensor_tensor(kids[:, :, :, 0], QQ[:, :, :], NS[:, :, 0:10], ALU.mult).then_inc(co_ok, 1)
            nc.vector.tensor_tensor(kids[:, :, :, 1], QQ[:, :, :], SG[:, :, 0:10], ALU.mult).then_inc(co_ok, 1)

            for k in range(NT // 2):
                dve.wait_ge(o_ps, k + 1)
                if k >= 4:
                    dve.wait_ge(out_ok[k // 2 % 2], 16 * (k // 4))
                nc.vector.tensor_tensor(OUTS[:, k % 4, :], BANK[4 + k % 2][:, 0:2 * D], HT[:, 2 * k:2 * k + 2, :].rearrange("p t d -> p (t d)"),
                                        ALU.add).then_inc(o_ok, 1)

        @block.tensor
        def _(pe):
            pe.wait_ge(ld_const, 16 * N_CONST)
            ja, jd = 0, 0

            def a_bank():
                if ja >= 4:
                    pe.wait_ge(act_a, ja - 3 + (1 if ja >= 20 + 4 else 0))
                return BANK[ja % 4]

            def d_bank():
                if jd >= 4:
                    pe.wait_ge(dve_d, jd - 3)
                return BANK[4 + jd % 4]

            pe.wait_ge(g2_in, 32)
            for b in range(B):
                bank = a_bank()
                for g in range(2):
                    ins = nc.tensor.transpose(bank[0:F2, g * P:(g + 1) * P], G2[:, g, b * F2:(b + 1) * F2], ID[:, :])
                ins.then_inc(pe_a, 1)
                ja += 1
            bank = a_bank()
            pe.wait_ge(act_a, 16)
            for g in range(GP):
                ins = nc.tensor.matmul(bank[0:EMB, 0:B * T2], W2S[:, g, :], G2T[:, g, :, :].rearrange("f b t -> f (b t)"), start=g == 0, stop=g == GP - 1)
            ins.then_inc(pe_a, 1)
            ja += 1
            pe.wait_ge(g1r_ok, 1)
            for q in range(4):
                bank = d_bank()
                for j in range(4):
                    ins = nc.tensor.transpose(bank[0:HALF, j * P:(j + 1) * P],
                                              G1R[:, 4 * q + j, :], ID[:, :])
                ins.then_inc(pe_d, 1)
                jd += 1
            bank = a_bank()
            pe.wait_ge(act_a, 17)
            for g in range(2):
                ins = nc.tensor.matmul(bank[:, g * D:(g + 1) * D], E2[:, g * P:(g + 1) * P], WFS[:, 2, :], start=True, stop=True)
            ins.then_inc(pe_a, 1)
            ja += 1
            nc.tensor.matmul(d_bank()[:, 0:D], BC[:, 0:1].broadcast_to([EMB, P]), WFS[:, 0, :], start=True, stop=True).then_inc(pe_d, 1)
            jd += 1
            nc.tensor.matmul(d_bank()[0:GP * F0, 0:D], W0S[:, :], WFS[:, 0, :], start=True, stop=True).then_inc(pe_d, 1)
            jd += 1
            pe.wait_ge(dve_d, 4)
            for c in range(2):
                bank = a_bank()
                for g in range(2):
                    ins = nc.tensor.matmul(bank[0:EMB, :], W1S[:, g, :], G1T[:, g, 8 * c:8 * c + 8, :].rearrange("f b t -> f (b t)"),
                                           start=g == 0, stop=g == 1)
                ins.then_inc(pe_a, 1)
                ja += 1
            pe.wait_ge(act_a, 20)
            for q in range(B // 2):
                bank = d_bank()
                for j in range(2):
                    b = 2 * q + j
                    ins = nc.tensor.matmul(bank[T1:P, j * D:(j + 1) * D], E1[:, b * T1:(b + 1) * T1], WFS[:, 1, :], start=True, stop=True)
                ins.then_inc(pe_d, 1)
                jd += 1
            for t in range(TT):
                pe.wait_ge(g0r_ok, t + 1)
                for q in range(4):
                    bank = a_bank()
                    for j in range(4):
                        b = 4 * q + j
                        ins = nc.tensor.transpose(bank[0:GP * F0, j * P:(j + 1) * P], G0R[:, t, b, :], ID[:, :])
                    ins.then_inc(pe_a, 1)
                    ja += 1
                if t == 0:
                    pe.wait_ge(ld_z2, 16 * B)
                    pe.wait_ge(ld_interp, 16)
                    pe.wait_ge(dve_d, 14)
                for q in range(B // 2):
                    bank = d_bank()
                    pe.wait_ge(act_a, 21 + 4 * t + q // 2 + 1)
                    for j in range(2):
                        b = 2 * q + j
                        ins = nc.tensor.matmul(bank[:, j * D:(j + 1) * D], LH[:, TT * b + t, :], RH[:, b, :], start=True, stop=True)
                    ins.then_inc(pe_d, 1)
                    jd += 1
            pe.wait_ge(act_a, 29)
            pe.wait_ge(dve_d, 30)

            def xn_t(b):
                pe.wait_ge(xn_ok, b.count(1, 1))
                if not (b.first or b.second):
                    pe.wait_ge(mt_ok, (b - 1).count(1))
                for k in range(2):
                    for t in range(TT):
                        ins = nc.tensor.transpose(BANK[MB][0:HALF, k * S + t * P:k * S + (t + 1) * P], XN[:, t, k * HALF:(k + 1) * HALF], ID[:, :])
                ins.then_inc(xt_ps, 1)

            def qk(b, w):
                pe.wait_ge(xnt_ok, b.count(1, 1))
                if w == 1:
                    pe.wait_ge(r_ok, b.count(2, 1))
                for m in range(2):
                    for k in range(2):
                        ins = nc.tensor.matmul(BANK[MB][0:HALF, m * S:(m + 1) * S], WA[:, k, (2 * w + m) * HALF:(2 * w + m + 1) * HALF],
                                               XNT[:, k, :], start=k == 0, stop=k == 1)
                ins.then_inc(qk_ps, 1)

            def v_proj(b):
                pe.wait_ge(r_ok, b.count(2, 2))
                for t in range(TT):
                    for k in range(2):
                        ins = nc.tensor.matmul(BANK[MB][:, t * D:(t + 1) * D], XNT[:, k, t * P:(t + 1) * P], WA[:, k, 2 * D:3 * D],
                                               start=k == 0, stop=k == 1)
                ins.then_inc(v_ps, 1)

            def scores(b, par, u):
                n = SU * par + u
                if b.first:
                    if u >= 2:
                        pe.wait_ge(max_ok, u - 1)
                else:
                    pe.wait_ge(max_ok, b.count(SU, u - 1))
                bank = BANK[S_BANK[n % 2]]
                if u < 3:
                    for j in range(4):
                        h = 4 * u + j
                        nc.tensor.matmul(bank[:, j * P:(j + 1) * P], QS[par][:, h, 0:P], KS[par][:, h, 0:P], start=j == 0, stop=False)
                    nc.tensor.matmul(bank[:, :], IDB[:, :], MASKQ[:, :, :].rearrange("p a k -> p (a k)"), start=False, stop=True).then_inc(s_ps, 1)
                else:
                    for j in range(2):
                        h = 2 * (u - 3) + j
                        nc.tensor.matmul(bank[:, j * S:(j + 1) * S], QS[par][:, h, P:S], KS[par][:, h, :], start=j == 0, stop=False)
                    nc.tensor.matmul(bank[:, :].rearrange("p (h k) -> p h k", h=2)[:, :, P:S], IDB[:, :], MASKQ[:, 0:2, :],
                                     start=False, stop=True).then_inc(s_ps, 1)

            def max_t(b):
                pe.wait_ge(mp_ok, b.count(1, 1))
                if not b.last:
                    pe.wait_ge(v_ok, b.count(1, 2))
                for t in range(TT):
                    ins = nc.tensor.transpose(BANK[MB][0:NM, t * P // 2:(t + 1) * P // 2].bitcast(bf16), MP[:, t, :, :].rearrange("p a h -> p (a h)"), IDB[:, :])
                ins.then_inc(mt_ps, 1)

            def scores_t(b, par, v):
                n = SU * par + v
                if b.first:
                    if v >= 2:
                        pe.wait_ge(exp_ok, v - 1)
                else:
                    pe.wait_ge(exp_ok, b.count(SU, v - 1))
                bank = BANK[T_BANK[n % 2]]
                g, r = v // 3, v % 3
                if r < 2:
                    hs = [4 * g + 2 * r, 4 * g + 2 * r + 1]
                    for j, h in enumerate(hs):
                        nc.tensor.matmul(bank[:, j * S:(j + 1) * S], KS[par][:, h, 0:P], QS[par][:, h, :], start=j == 0, stop=False)
                    for j, h in enumerate(hs):
                        nc.tensor.matmul(bank[:, j * S:(j + 1) * S], SEL[:, h, :], MT[:, :], start=False, stop=False)
                    nc.tensor.matmul(bank[:, :].rearrange("p (h k) -> p h k", h=2)[:, :, 0:P], IDB[:, :], MASKK[:, 0:2, :],
                                     start=False, stop=True).then_inc(st_ps, 1)
                else:
                    for j in range(4):
                        h = 4 * g + j
                        nc.tensor.matmul(bank[:, j * P:(j + 1) * P], KS[par][:, h, P:S], QS[par][:, h, P:S], start=j == 0, stop=False)
                    for j in range(4):
                        nc.tensor.matmul(bank[:, j * P:(j + 1) * P], SEL[:, 4 * g + j, :], MT[:, P:S], start=False, stop=False)
                    nc.tensor.matmul(bank[:, :], IDB[:, :], MASKK[:, :, :].rearrange("p a k -> p (a k)"), start=False, stop=True).then_inc(st_ps, 1)

            def weighted(b, par, g):
                pe.wait_ge(exp_ok, b.count(SU, 3 * g + 3))
                if g == 0 and not b.first:
                    pe.wait_ge(ot_ok, (b - 1).count(2, 1))
                if g == 2 and not b.first:
                    pe.wait_ge(ot_ok, b.count(2))
                if g == 0:
                    pe.wait_ge(v_ok, b.count(1, 1))
                bank = BANK[O_BANK[g // 2]]
                c = (g % 2) * S
                for j in range(4):
                    nc.tensor.matmul(bank[32 * j:32 * j + 32, c:c + S], VA[par][:, 0, 4 * g + j, :],
                                     PT[:, 3 * g + j // 2, (j % 2) * S:(j % 2 + 1) * S], start=True, stop=False, skip_group_check=True)
                for j in range(4):
                    ins = nc.tensor.matmul(bank[32 * j:32 * j + 32, c + P:c + S], VA[par][:, 1, 4 * g + j, :],
                                           PT[:, 3 * g + 2, j * P:(j + 1) * P], start=False, stop=True, skip_group_check=True)
                ins.then_inc(av_ps, 1)

            def out_t(b, t):
                pe.wait_ge(ot_ok, b.count(2, 2))
                if t == 1:
                    pe.wait_ge(on_ok, b.count(2, 1))
                elif b.last:
                    pe.wait_ge(h2_ok, b.count(2))
                for g in range(3):
                    ins = nc.tensor.transpose(BANK[MA][:, g * P:(g + 1) * P], OT[:, g, t * P:(t + 1) * P], ID[:, :])
                ins.then_inc(t1_ps, 1)

            def on_t(b):
                pe.wait_ge(on_ok, b.count(2, 2))
                for k in range(2):
                    for t in range(TT):
                        ins = nc.tensor.transpose(BANK[MA][0:HALF, k * S + t * P:k * S + (t + 1) * P], ON[:, t, k * HALF:(k + 1) * HALF], ID[:, :])
                ins.then_inc(t2_ps, 1)

            def project(b):
                pe.wait_ge(ont_ok, b.count(1, 1))
                for t in range(TT):
                    for k in range(2):
                        ins = nc.tensor.matmul(BANK[MA][:, t * D:(t + 1) * D], ONT[:, k, t * P:(t + 1) * P], WP[:, k, :], start=k == 0, stop=k == 1)
                ins.then_inc(pj_ps, 1)

            def step(b, par, has_front, has_back):
                pe.wait_ge(stacked, (b + 1).count(12 * 16))
                scores(b, par, 0)
                if has_back:
                    weighted(b - 1, 1 - par, 2)
                scores(b, par, 1)
                if has_front:
                    xn_t(b + 1)
                scores(b, par, 2)
                if has_back:
                    out_t(b - 1, 0)
                scores(b, par, 3)
                if has_front:
                    qk(b + 1, 0)
                scores(b, par, 4)
                if has_back:
                    out_t(b - 1, 1)
                scores(b, par, 5)
                if has_front:
                    qk(b + 1, 1)
                scores(b, par, 6)
                if has_back:
                    on_t(b - 1)
                scores(b, par, 7)
                scores(b, par, 8)
                if has_front:
                    v_proj(b + 1)
                if has_back:
                    project(b - 1)
                max_t(b)
                pe.wait_ge(mt_ok, b.count(1, 1))
                for v in range(6):
                    scores_t(b, par, v)
                weighted(b, par, 0)
                for v in range(6, 9):
                    scores_t(b, par, v)
                weighted(b, par, 1)

            xn_t(Image(0, 0))
            qk(Image(0, 0), 0)
            qk(Image(0, 0), 1)
            v_proj(Image(0, 0))
            pe.wait_ge(v_ok, 1)
            step(Image(0, 0), 0, True, False)
            with pe.Fori(0, (B - 2) // 2) as i:
                step(Image(i, 1), 1, True, True)
                step(Image(i, 2), 0, True, True)
            step(Image(0, B - 1), 1, False, True)
            last = Image(0, B - 1)
            weighted(last, 1, 2)
            out_t(last, 0)
            out_t(last, 1)
            on_t(last)
            project(last)

            def logits(k):
                pe.wait_ge(x2t_ok, k + 1)
                if k % 8 == 0 and k >= 16:
                    pe.wait_ge(lg_ok, k // 8 - 1)
                for c in range(2):
                    ins = nc.tensor.matmul(BANK[4 + (k // 8) % 2][:, (k % 8) * NODES:(k % 8 + 1) * NODES], X2T[k % 4][:, c, :], WIN[:, c, :],
                                           start=c == 0, stop=c == 1)
                ins.then_inc(lg_ps, 1)

            for k in range(NT):
                pe.wait_ge(x2_ok, k + 1)
                if k >= 2:
                    pe.wait_ge(x2t_ok, k - 1)
                for c in range(2):
                    ins = nc.tensor.transpose(BANK[k % 2][0:HALF, c * P:(c + 1) * P], X2[:, k % 4, c * HALF:(c + 1) * HALF], ID[:, :])
                ins.then_inc(x2t_ps, 1)
                if k >= 1:
                    logits(k - 1)
            logits(NT - 1)

            def output(k):
                pe.wait_ge(cot_ok, k + 1)
                if k % 2 == 0 and k >= 4:
                    pe.wait_ge(o_ok, k // 2 - 1)
                ins = nc.tensor.matmul(BANK[4 + (k // 2) % 2][:, (k % 2) * D:(k % 2 + 1) * D], COT[k % 4][:, :], WEX[:, :], start=True, stop=True)
                if k % 2:
                    ins.then_inc(o_ps, 1)

            pe.wait_ge(co_ok, 2)
            pe.wait_ge(lg_ok, NT // 8)
            pe.wait_ge(va_init, 5)
            for k in range(NT):
                if k >= 2:
                    pe.wait_ge(cot_ok, k - 1)
                nc.tensor.transpose(BANK[k % 2][0:NCO, 0:P], CO[:, k, :], ID[:, :]).then_inc(cot_ps, 1)
                if k >= 1:
                    output(k - 1)
            output(NT - 1)


def _interp(length):
    import numpy as np
    pos = np.clip((np.arange(S, dtype=np.float32) + np.float32(0.5)) * np.float32(length / S) - np.float32(0.5), 0, length - 1)
    lo = np.floor(pos).astype(np.int32)
    hi = np.minimum(lo + 1, length - 1)
    w = (pos - lo).astype(np.float32)
    m = np.zeros((length, S), np.float32)
    np.add.at(m, (lo, np.arange(S)), np.float32(1) - w)
    np.add.at(m, (hi, np.arange(S)), w)
    return m


def kernel(x, L0_tok_W0, L0_tok_b0, L0_tok_W1, L0_tok_b1, L0_tok_W2, L0_tok_b2, L0_tok_Wf, L0_tok_bf,
           L0_tok_idx0, L0_tok_idx1, L0_tok_idx2, L0_attn_W_attn, L0_attn_b_attn, L0_attn_W_proj, L0_attn_b_proj,
           L0_ffn_weights_in, L0_ffn_weights_out):
    import numpy as np
    import concourse.bacc as bacc
    from concourse.bass_utils import run_bass_kernel_spmd

    x = np.asarray(x)

    def patches(p):
        h = IMG // p
        t = x.reshape(B, CH, h, p, h, p).transpose(2, 4, 0, 3, 5, 1)
        return t.reshape(h * h, B * p * p * CH)

    i0, i1, i2 = (np.asarray(i) for i in (L0_tok_idx0, L0_tok_idx1, L0_tok_idx2))
    wout = np.asarray(L0_ffn_weights_out)
    bf16 = mybir.dt.np(mybir.dt.bfloat16)
    tri = np.tril(np.ones((P, P), bool))
    masked = np.float32(-2.0 ** 126)
    select = np.zeros((NM, H, P), np.float32)
    for part in range(2):
        for h in range(H):
            select[part * H + h, h, :] = 1
    arrays = {
        "x0": patches(1), "x1": patches(2), "x2": patches(4),
        "ix0": i0.reshape(TT, P, GP).transpose(1, 0, 2).reshape(P, TT * GP),
        "ix1": i1.reshape(T1, 2, GP // 2).transpose(1, 0, 2).reshape(P, GP // 2),
        "ix2": i2.reshape(T2, 2, GP // 2).transpose(2, 0, 1).reshape(P, 2),
        "w0": np.asarray(L0_tok_W0), "w1t": np.asarray(L0_tok_W1).T, "w2t": np.asarray(L0_tok_W2).T,
        "wft": np.asarray(L0_tok_Wf).T, "bcol": np.stack([np.asarray(v) for v in (L0_tok_b0, L0_tok_b1, L0_tok_b2)], 1),
        "bf": np.asarray(L0_tok_bf),
        "wa": np.asarray(L0_attn_W_attn), "bqk": np.asarray(L0_attn_b_attn)[:2 * D].reshape(4, HALF).T,
        "bv": np.asarray(L0_attn_b_attn)[2 * D:],
        "wp": np.asarray(L0_attn_W_proj), "bp": np.asarray(L0_attn_b_proj),
        "wint": np.asarray(L0_ffn_weights_in).T,
        "wext": wout[np.array(list(range(NODES)) + [NODES - 1] * (NCO - NODES))],
        "identf": np.eye(P, dtype=np.float32), "identb": np.eye(P, dtype=np.float32).astype(bf16),
        "maskq": np.where(tri, np.float32(0), masked).astype(bf16),
        "maskk": np.where(tri.T, np.float32(0), masked).astype(bf16),
        "sel": select.astype(bf16),
        "interp": np.concatenate([_interp(T2), _interp(T1)]),
    }
    arrays = {n: np.ascontiguousarray(a) for n, a in arrays.items()}
    nc = bacc.Bacc("TRN2", target_bir_lowering=False, num_devices=1)
    args = [nc.dram_tensor(n, a.shape, mybir.dt.from_np(a.dtype), kind="ExternalInput").ap() for n, a in arrays.items()]
    out = nc.dram_tensor("out", (B * S, D), mybir.dt.float32, kind="ExternalOutput").ap()
    parts = nc.dram_tensor("parts", (B, PARTS, 4, HALF, S), mybir.dt.bfloat16, kind="Internal").ap()
    vit_tower_kernel(nc, *args, out, parts)
    r = run_bass_kernel_spmd(nc, [arrays], core_ids=[0])
    return r.results[0]["out"].reshape(B, S, D)
```

```python
import concourse.bass as bass
from concourse import mybir
from contextlib import ExitStack

B, CH, IMG = 16, 3, 64
GP, EMB = 16, 64
D = 3 * EMB
S = IMG * IMG // GP
P = 128
TT = S // P
NT = B * TT
H, HS = 12, 16
HALF = D // 2
F0, F1, F2 = CH, 4 * CH, 16 * CH
T1, T2 = S // 4, S // 16
NODES = 21
NCO = 32
EPS = 1e-5
PARTS = 3
KQ = 6 * HS
KM = KQ + 2
G = 3
HG = H // G
SU = 9
SCALE = 0.25


class Image:

    def __init__(self, pair, off):
        self.pair, self.off = pair, off
        number = off if isinstance(pair, int) else None
        self.first, self.second, self.last = number == 0, number == 1, number == B - 1

    def __add__(self, n):
        return Image(self.pair, self.off + n)

    def __sub__(self, n):
        return Image(self.pair, self.off - n)

    def count(self, per, more=0):
        return self.pair * (2 * per) + (self.off * per + more)


def vit_tower_kernel(nc, x0, x1, x2, ix0, ix1, ix2, w0, w1t, w2t, wft, bcol, bf,
                     wa, bqk, bv, wp, bp, wint, wext, identf, identb, maskq, interp,
                     out, parts):
    fp32, bf16, i32 = mybir.dt.float32, mybir.dt.bfloat16, mybir.dt.int32
    ALU = mybir.AluOpType
    ACT = mybir.ActivationFunctionType
    AX = mybir.AxisListType

    ctx = ExitStack()
    with ctx:
        def sb(name, shape, dt=fp32):
            return ctx.enter_context(nc.sbuf_tensor(name, shape, dt))

        def sem(name):
            return ctx.enter_context(nc.semaphore(name))

        ID = sb("ID", [P, P])
        CARRY = sb("CARRY", [1, 2])
        IDB = sb("IDB", [P, P], bf16)
        MASKQ = sb("MASKQ", [P, 4, P], bf16)
        W0S = sb("W0S", [EMB, GP * F0])
        W1S = sb("W1S", [HALF, 2, EMB])
        W2S = sb("W2S", [F2, GP, EMB])
        WFS = sb("WFS", [EMB, 3, D])
        WA = sb("WA", [HALF, 2, 3 * D])
        WP = sb("WP", [HALF, 2, D])
        WIN = sb("WIN", [HALF, 2, NODES])
        WEX = sb("WEX", [NCO, D])
        BC = sb("BC", [EMB, 3])
        BFB = sb("BFB", [P, D])
        BQK = sb("BQK", [HALF, 4])
        BV = sb("BV", [P, D])
        BP = sb("BP", [P, D])

        I0 = sb("I0", [P, TT * GP], i32)
        I1 = sb("I1", [P, GP // 2], i32)
        I2 = sb("I2", [P, 2], i32)
        CB = sb("CB", [P, D])
        C0 = sb("C0", [GP * F0, D])
        HT = sb("HT", [P, NT, D])
        ST = sb("ST", [P, NT, 6])
        MV = sb("MV", [P, NT, 2])
        VE = sb("VE", [P, NT])
        SD = sb("SD", [P, NT])
        RSTD = sb("RSTD", [P, NT])
        NMR = sb("NMR", [P, NT])

        XN = sb("XN", [P, TT, D])
        XNT = sb("XNT", [HALF, 2, S])
        PART = [sb(f"PART{i}", [HALF, 4, S], bf16) for i in range(PARTS)]
        RES = sb("RES", [HALF, 4, S])
        QS = [sb(f"QS{i}", [KM, H, S], bf16) for i in range(2)]
        KS = [sb(f"KS{i}", [KM, H, S], bf16) for i in range(2)]
        VA = [sb(f"VA{i}", [P, TT, H, 32]) for i in range(2)]
        MX = sb("MX", [P, TT, H])
        MP = sb("MP", [P, G, TT, 2, HG], bf16)
        MT = sb("MT", [2 * HG, G, S], bf16)
        OT = sb("OT", [P, 3, S])
        RC = sb("RC", [P, TT, H])
        ON = sb("ON", [P, TT, D])
        ONT = sb("ONT", [HALF, 2, S])
        H2 = sb("H2", [P, TT, D])
        MV2 = sb("MV2", [P, TT, 2])
        ST2 = sb("ST2", [P, TT, 6])

        CO = sb("CO", [P, NT, NCO])
        with ExitStack() as early:
            tok = lambda name, shape, dt=fp32: early.enter_context(nc.sbuf_tensor(name, shape, dt))
            G0 = tok("G0", [P, TT, GP, B * F0])
            G1 = tok("G1", [P, GP // 2, B * F1])
            G2 = tok("G2", [P, 2, B * F2])
            G0R = tok("G0R", [P, TT, B, GP * F0])
            G1R = tok("G1R", [P, B, HALF])
            G1T = tok("G1T", [HALF, 2, B, T1])
            G2T = tok("G2T", [F2, GP, B, T2])
            E1 = tok("E1", [EMB, B * T1])
            E2 = tok("E2", [EMB, B * T2])
            Z2 = tok("Z2", [P, 2, D])
            LH = tok("LH", [P, NT, P])
            RH = tok("RH", [P, B, D])

        PT = sb("PT", [P, SU, 512])

        X2 = sb("X2", [P, 4, D])
        X2T = [sb(f"X2T{i}", [HALF, 2, P]) for i in range(4)]
        LG = sb("LG", [P, NT, NODES])
        GE = sb("GE", [P, NT, NODES])
        SG = sb("SG", [P, NT, NODES])
        NS = sb("NS", [P, NT, NODES])
        RE = sb("RE", [P, NT, 22])
        QQ = sb("QQ", [P, NT, 10])
        COT = [sb(f"COT{i}", [NCO, P]) for i in range(4)]
        OUTS = sb("OUTS", [P, 4, 2 * D])

        BANK = [ctx.enter_context(nc.psum_tensor(f"bank{i}", [P, 512], fp32)) for i in range(8)]

        ld_idx, ld_const, ld_interp, ld_z2 = sem("ld_idx"), sem("ld_const"), sem("ld_interp"), sem("ld_z2")
        g2_in, g1_in = sem("g2_in"), sem("g1_in")
        g1r_ok, g0r_ok = sem("g1r_ok"), sem("g0r_ok")
        g0_in = [sem(f"g0_in{t}") for t in range(TT)]
        pe_a, pe_d = sem("pe_a"), sem("pe_d")
        act_a, dve_d = sem("act_a"), sem("dve_d")
        va_init = sem("va_init")
        stat, var_ok, sd_ok, rstd_ok, nmr_ok = sem("stat"), sem("var_ok"), sem("sd_ok"), sem("rstd_ok"), sem("nmr_ok")
        xn_ok, xt_ps, xnt_ok, qk_ps, p0_ok, r_ok, p1_ok, p2_ok = [
            sem(n) for n in ("xn_ok", "xt_ps", "xnt_ok", "qk_ps", "p0_ok", "r_ok", "p1_ok", "p2_ok")]
        stored, stacked = sem("stored"), sem("stacked")
        v_ps, v_ok = sem("v_ps"), sem("v_ok")
        s_ps, max_ok, mh_ok, mp_ok, mt_ps, mt_ok = [
            sem(n) for n in ("s_ps", "max_ok", "mh_ok", "mp_ok", "mt_ps", "mt_ok")]
        st_ps, exp_ok, av_ps, ot_ok, m_in, cut_ok, carried = [sem(n) for n in ("st_ps", "exp_ok", "av_ps", "ot_ok", "m_in", "cut_ok", "carried")]
        t1_ps, rc_ok, on_ok, t2_ps, ont_ok, pj_ps, h2_ok = [
            sem(n) for n in ("t1_ps", "rc_ok", "on_ok", "t2_ps", "ont_ok", "pj_ps", "h2_ok")]
        st2_ok, mv2_ok, mvh_ok = sem("st2_ok"), sem("mv2_ok"), sem("mvh_ok")
        x2_ok, x2t_ps, x2t_ok, lg_ps, lg_ok, ge_ok, tree = [
            sem(n) for n in ("x2_ok", "x2t_ps", "x2t_ok", "lg_ps", "lg_ok", "ge_ok", "tree")]
        co_ok, cot_ps, cot_ok, o_ps, o_ok = [
            sem(n) for n in ("co_ok", "cot_ps", "cot_ok", "o_ps", "o_ok")]
        out_ok = [sem(f"out_ok{n}") for n in range(2)]

        N_CONST = 16
        S_BANK = [0, 1]
        T_BANK = [2, 3]
        O_BANK = [4, 5]
        MA, MB = 6, 7

        block = ctx.enter_context(nc.Block())

        @block.sync
        def _(sp):
            for t, src in ((I2, ix2), (I1, ix1), (I0, ix0)):
                sp.dma_start(t[:, :], src).then_inc(ld_idx, 16)
            sp.dma_start(ID[:, :], identf).then_inc(ld_const, 16)
            sp.dma_start(W2S[:, :, :], w2t.rearrange("(g f) e -> f g e", g=GP)).then_inc(ld_const, 16)
            sp.dma_start(W1S[:, :, :], w1t.rearrange("(g f) e -> f g e", g=2)).then_inc(ld_const, 16)
            sp.dma_start(WFS[:, :, :], wft.rearrange("(l e) o -> e l o", l=3)).then_inc(ld_const, 16)
            sp.dma_start(W0S[:, :], w0).then_inc(ld_const, 16)
            sp.dma_start(BC[:, :], bcol).then_inc(ld_const, 16)
            for t, src in ((BFB, bf), (BV, bv), (BP, bp)):
                sp.dma_start(t[:, :], src.rearrange("(a n) -> a n", a=1).broadcast_to([P, D])).then_inc(ld_const, 16)
            sp.dma_start(LH[GP * F0:P, :, :].rearrange("k (b t) n -> k b (t n)", b=B),
                         interp.rearrange("k (a n) -> k a n", a=1).broadcast_to([T2 + T1, B, S])).then_inc(ld_interp, 16)
            sp.dma_start(BQK[:, :], bqk).then_inc(ld_const, 16)
            sp.dma_start(WA[:, :, :], wa.rearrange("(k p) n -> p k n", k=2)).then_inc(ld_const, 16)
            sp.dma_start(WP[:, :, :], wp.rearrange("(k p) n -> p k n", k=2)).then_inc(ld_const, 16)
            sp.dma_start(WIN[:, :, :], wint.rearrange("(k p) n -> p k n", k=2)).then_inc(ld_const, 16)
            sp.dma_start(WEX[:, :], wext).then_inc(ld_const, 16)
            sp.dma_start(IDB[:, :], identb).then_inc(ld_const, 16)
            sp.dma_start(MASKQ[:, :, :], maskq.rearrange("q (a k) -> q a k", a=1).broadcast_to([P, 4, P])).then_inc(ld_const, 16)
            sp.wait_ge(act_a, 18)
            for b in range(B):
                r = (b % 8) * T2
                sp.dma_start(RH[GP * F0:GP * F0 + T2, b, :], Z2[r:r + T2, b // 8, :]).then_inc(ld_z2, 16)

            def restack(b, par):
                def fixed(value):
                    return value if isinstance(value, int) else sp.snap(value)

                image, part0, part12 = fixed(b.count(1)), fixed(b.count(2, 2)), fixed(b.count(1, 1))
                in_dram = fixed(b.count(16 * PARTS, 16 * PARTS))
                for n, (ready, value) in enumerate(((p0_ok, part0), (p1_ok, part12), (p2_ok, part12))):
                    sp.wait_ge(ready, value)
                    sp.dma_start(parts[bass.ds(image, 1), n, :, :, :].rearrange("a m p s -> p (a m) s"),
                                 PART[n][:, :, :]).then_inc(stored, 16)
                sp.wait_ge(stored, in_dram)
                view = parts[bass.ds(image, 1), :, :, :, :].rearrange("a n (w m) p s -> (a n) w (m p s)", w=2)
                for w, dst in ((0, QS[par]), (1, KS[par])):
                    row = 0
                    for n in (3, 2, 1):
                        src = view[0:n, w, :] if w else view[3 - n:4 - n, w, :].broadcast_to([n, H * HS * S])
                        sp.dma_start(dst[row:row + n * HS, :, :].rearrange("r h s -> r (h s)"),
                                     src.rearrange("n (d c) -> n d c", d=HS)).then_inc(stacked, 16)
                        row += n * HS

            for par in range(2):
                restack(Image(0, par), par)
            with sp.Fori(0, (B - 2) // 2) as i:
                for par in range(2):
                    restack(Image(i, 2 + par), par)

            for k in range(NT // 4):
                sp.wait_ge(o_ok, 2 * k + 2)
                sp.dma_start(out[4 * k * P:(4 * k + 4) * P, :].rearrange("(t p) d -> p t d", p=P),
                             OUTS[:, 2 * (k % 2):2 * (k % 2) + 2, :].rearrange("p a (t d) -> p (a t) d", d=D)).then_inc(out_ok[k % 2], 16)
            for n in range(2):
                sp.wait_ge(out_ok[n], 16 * (NT // 8))

        @block.gpsimd
        def _(pool):
            pool.wait_ge(ld_idx, 48)
            for j in range(2):
                pool.indirect_dma_start(G2[:, j, :], None, x2, bass.IndirectOffsetOnAxis(ap=I2[:, j:j + 1], axis=0)).then_inc(g2_in, 16)
            for j in range(GP // 2):
                pool.indirect_dma_start(G1[:, j, :], None, x1, bass.IndirectOffsetOnAxis(ap=I1[:, j:j + 1], axis=0)).then_inc(g1_in, 16)
            for t in range(TT):
                for g in range(GP):
                    j = t * GP + g
                    pool.indirect_dma_start(G0[:, t, g, :], None, x0, bass.IndirectOffsetOnAxis(ap=I0[:, j:j + 1], axis=0)).then_inc(g0_in[t], 16)
            for i in range(2):
                pool.memset(VA[i][:, :, :, HS:32], 0.0).then_inc(va_init, 1)
            pool.wait_ge(va_init, 2)
            for i in range(2):
                pool.memset(VA[i][:, :, :, HS:HS + 1], 1.0).then_inc(va_init, 1)
                pool.wait_ge(va_init, 3 + 2 * i)
                pool.memset(KS[i][KQ:KM, :, :], 1.0).then_inc(va_init, 1)
                pool.wait_ge(va_init, 4 + 2 * i)
            pool.memset(CARRY[:, :], 0.0).then_inc(va_init, 1)
            pool.memset(CO[:, :, 0:1], 0.0).then_inc(va_init, 1)
            pool.wait_ge(va_init, 8)

            def low(b):
                pool.wait_ge(p1_ok, b.count(1, 1))
                pool.tensor_tensor(PART[2][:, :, :], RES[:, :, :], PART[1][:, :, :], ALU.subtract).then_inc(p2_ok, 1)

            def causal(b, g):
                for r in range(3):
                    if r != 1:
                        n = 2 * g + (r == 2)
                        if not (b.first and n == 0):
                            pool.wait_ge(carried, b.count(6, n))
                        pool.wait_ge(exp_ok, b.count(SU, 3 * g + (2 if r == 0 else 3)))
                        pool.tensor_tensor(CARRY[:, 1:2], CARRY[:, 0:1], CARRY[:, 0:1], ALU.add).then_inc(carried, 1)
                    n = 2 if r < 2 else 4
                    e = PT[:, 3 * g + r, :].rearrange("p (h q) -> p h q", h=n)[:, :, 0:P]
                    pool.affine_select(out=e, in_=e, compare_op=ALU.is_ge, fill=0.0, base=0,
                                       pattern=[[0, n], [1, P]], channel_multiplier=-1).then_inc(cut_ok, 1)

            def step(b, has_front, has_back):
                if has_back:
                    causal(b - 1, 2)
                if has_front:
                    low(b + 1)
                causal(b, 0)
                causal(b, 1)

            low(Image(0, 0))
            step(Image(0, 0), True, False)
            with pool.Fori(0, (B - 2) // 2) as i:
                step(Image(i, 1), True, True)
                step(Image(i, 2), True, True)
            step(Image(0, B - 1), False, True)
            causal(Image(0, B - 1), 2)

        @block.scalar
        def _(act):
            act.wait_ge(ld_const, 16 * N_CONST)
            job = 0

            def a_bank():
                return BANK[job % 4]

            for b in range(B):
                act.wait_ge(pe_a, job + 1)
                nc.scalar.copy(G2T[:, :, b, :], a_bank()[0:F2, 0:2 * P].rearrange("f (g t) -> f g t", t=T2)).then_inc(act_a, 1)
                job += 1
            act.wait_ge(pe_a, job + 1)
            nc.scalar.activation(E2[:, :], a_bank()[0:EMB, 0:B * T2], ACT.Identity, bias=BC[:, 2:3]).then_inc(act_a, 1)
            job += 1
            act.wait_ge(pe_a, job + 1)
            nc.scalar.copy(Z2[:, :, :], a_bank()[:, 0:2 * D].rearrange("p (a d) -> p a d", a=2)).then_inc(act_a, 1)
            job += 1
            for c in range(2):
                act.wait_ge(pe_a, job + 1)
                nc.scalar.activation(E1[:, c * 512:(c + 1) * 512], a_bank()[0:EMB, :], ACT.Identity, bias=BC[:, 1:2]).then_inc(act_a, 1)
                job += 1
            act.wait_ge(dve_d, 6)
            nc.scalar.copy(RH[0:GP * F0, :, :], C0[:, :].rearrange("p (a d) -> p a d", a=1).broadcast_to([GP * F0, B, D])).then_inc(act_a, 1)
            act_extra = 1
            for t in range(TT):
                for q in range(4):
                    act.wait_ge(pe_a, job + 1)
                    nc.scalar.copy(LH[0:GP * F0, :, :].rearrange("k (b t) n -> k b t n", t=TT)[:, 4 * q:4 * q + 4, t, :],
                                   a_bank()[0:GP * F0, :].rearrange("k (b n) -> k b n", b=4)).then_inc(act_a, 1)
                    job += 1
            act.wait_ge(var_ok, 1)
            nc.scalar.activation(SD[:, :], VE[:, :], ACT.Sqrt).then_inc(sd_ok, 1)

            def front(b):
                act.wait_ge(xt_ps, b.count(1, 1))
                nc.scalar.copy(XNT[:, :, :], BANK[MB][0:HALF, :].rearrange("p (k s) -> p k s", k=2)).then_inc(xnt_ok, 1)

            def first_part(b, w):
                act.wait_ge(qk_ps, b.count(2, w + 1))
                if w == 0 and not b.first:
                    act.wait_ge(stored, b.count(16 * PARTS))
                for m in range(2):
                    ins = nc.scalar.activation(PART[0][:, 2 * w + m, :], BANK[MB][0:HALF, m * S:(m + 1) * S],
                                               ACT.Identity, bias=BQK[:, 2 * w + m:2 * w + m + 1])
                ins.then_inc(p0_ok, 1)

            def outputs_t(b):
                act.wait_ge(t2_ps, b.count(1, 1))
                nc.scalar.copy(ONT[:, :, :], BANK[MA][0:HALF, :].rearrange("p (k s) -> p k s", k=2)).then_inc(ont_ok, 1)

            def out_group(b, late):
                if not b.first and not late:
                    act.wait_ge(t1_ps, b.count(2))
                if late:
                    act.wait_ge(av_ps, b.count(3, 3))
                    nc.scalar.copy(OT[:, 2, :], BANK[O_BANK[1]][:, 0:S]).then_inc(ot_ok, 1)
                else:
                    act.wait_ge(av_ps, b.count(3, 2))
                    nc.scalar.copy(OT[:, 0:2, :], BANK[O_BANK[0]][:, :].rearrange("p (g s) -> p g s", g=2)).then_inc(ot_ok, 1)

            def exps(b, par, g):
                for v in range(3 * g, 3 * g + 3):
                    act.wait_ge(st_ps, b.count(SU, v + 1))
                    if not b.first and v % 3 == 0:
                        act.wait_ge(av_ps, (b - 1).count(3, g + 1))
                    nc.scalar.activation(PT[:, v, :], BANK[T_BANK[(SU * par + v) % 2]][:, :], ACT.Exp, scale=SCALE).then_inc(exp_ok, 1)

            def maxima(b, par, g):
                act.wait_ge(mt_ps, b.count(G, g + 1))
                bank = MA if g == 0 else MB
                nc.scalar.copy(MT[:, g, :], BANK[bank][0:2 * HG, 0:S // 2].bitcast(bf16)).then_inc(mt_ok, 1)
                act.wait_ge(mt_ok, b.count(G, g + 1))
                for part in range(2):
                    act.dma_start(QS[par][KQ + part:KQ + part + 1, HG * g:HG * (g + 1), :],
                                  MT[HG * part:HG * (part + 1), g, :]).then_inc(m_in, 16)

            def step(b, par, has_front, has_back):
                if has_front:
                    front(b + 1)
                if has_back:
                    out_group(b - 1, False)
                if has_front:
                    first_part(b + 1, 0)
                if has_back:
                    exps(b - 1, 1 - par, 2)
                maxima(b, par, 0)
                if has_front:
                    first_part(b + 1, 1)
                if has_back:
                    out_group(b - 1, True)
                exps(b, par, 0)
                maxima(b, par, 1)
                if has_back:
                    outputs_t(b - 1)
                exps(b, par, 1)
                maxima(b, par, 2)

            front(Image(0, 0))
            first_part(Image(0, 0), 0)
            first_part(Image(0, 0), 1)
            step(Image(0, 0), 0, True, False)
            with act.Fori(0, (B - 2) // 2) as i:
                step(Image(i, 1), 1, True, True)
                step(Image(i, 2), 0, True, True)
            step(Image(0, B - 1), 1, False, True)
            last = Image(0, B - 1)
            out_group(last, False)
            exps(last, 1, 2)
            out_group(last, True)
            outputs_t(last)

            act.wait_ge(var_ok, 2)
            nc.scalar.activation(SD[:, :], VE[:, :], ACT.Sqrt).then_inc(sd_ok, 1)
            for k in range(NT):
                act.wait_ge(x2t_ps, k + 1)
                if k >= 4:
                    act.wait_ge(lg_ps, k - 3)
                nc.scalar.copy(X2T[k % 4][:, :, :], BANK[k % 2][0:HALF, 0:2 * P].rearrange("p (k s) -> p k s", k=2)).then_inc(x2t_ok, 1)
            act.wait_ge(lg_ok, NT // 8)
            nc.scalar.activation(GE[:, :, :], LG[:, :, :], ACT.Gelu).then_inc(ge_ok, 1)
            for k in range(NT):
                act.wait_ge(cot_ps, k + 1)
                if k >= 4:
                    act.wait_ge(o_ps, (k - 4) // 2 + 1)
                nc.scalar.copy(COT[k % 4][:, :], BANK[k % 2][0:NCO, 0:P]).then_inc(cot_ok, 1)

        @block.vector
        def _(dve):
            dve.wait_ge(ld_const, 16 * N_CONST)
            job = 0

            def d_bank():
                return BANK[4 + job % 4]

            dve.wait_ge(g1_in, 16 * (GP // 2))
            nc.vector.tensor_copy(G1R[:, :, :].rearrange("p b (g f) -> p g b f", f=F1), G1[:, :, :].rearrange("p g (b f) -> p g b f", f=F1)).then_inc(g1r_ok, 1)
            for q in range(4):
                dve.wait_ge(pe_d, job + 1)
                nc.vector.tensor_copy(G1T[:, :, 4 * q:4 * q + 4, :],
                                      d_bank()[0:HALF, :].rearrange("p (b g t) -> p g b t", b=4, g=2)).then_inc(dve_d, 1)
                job += 1
            dve.wait_ge(pe_d, job + 1)
            nc.vector.tensor_tensor(CB[:, :], d_bank()[:, 0:D], BFB[:, :], ALU.add).then_inc(dve_d, 1)
            job += 1
            dve.wait_ge(pe_d, job + 1)
            nc.vector.tensor_copy(C0[:, :], d_bank()[0:GP * F0, 0:D]).then_inc(dve_d, 1)
            job += 1
            dve.wait_ge(dve_d, 6)
            for q in range(B // 2):
                dve.wait_ge(pe_d, job + 1)
                nc.vector.tensor_tensor(RH[T1:P, 2 * q:2 * q + 2, :], d_bank()[T1:P, 0:2 * D].rearrange("p (b d) -> p b d", b=2),
                                        CB[T1:P, :].rearrange("p (a d) -> p a d", a=1).broadcast_to([T1, 2, D]), ALU.add).then_inc(dve_d, 1)
                job += 1
            done = 0
            for t in range(TT):
                dve.wait_ge(g0_in[t], 16 * GP)
                nc.vector.tensor_copy(G0R[:, t, :, :].rearrange("p b (g f) -> p g b f", f=F0),
                                      G0[:, t, :, :].rearrange("p g (b f) -> p g b f", f=F0)).then_inc(g0r_ok, 1)
                for q in range(B // 2):
                    dve.wait_ge(pe_d, job + 1)
                    view = HT[:, :, :].rearrange("p (b t) d -> p b t d", t=TT)[:, 2 * q:2 * q + 2, t, :]
                    nc.vector.tensor_copy(view, d_bank()[:, 0:2 * D].rearrange("p (b d) -> p b d", b=2)).then_inc(dve_d, 1)
                    job += 1
                    dve.wait_ge(dve_d, job)
                    for b in (2 * q, 2 * q + 1):
                        nc.vector.bn_stats(ST[:, TT * b + t, :], HT[:, TT * b + t, :]).then_inc(stat, 1)
                        done += 1
            dve.wait_ge(stat, NT)
            for k in range(NT):
                nc.vector.bn_aggr(MV[:, k, :], ST[:, k, :]).then_inc(stat, 1)

            def rstd(round_):
                nc.vector.tensor_scalar(VE[:, :], MV[:, :, 1], EPS, None, ALU.add).then_inc(var_ok, 1)
                dve.wait_ge(sd_ok, round_)
                nc.vector.reciprocal(RSTD[:, :], SD[:, :]).then_inc(rstd_ok, 1)
                dve.wait_ge(rstd_ok, round_)
                nc.vector.scalar_tensor_tensor(NMR[:, :], MV[:, :, 0], -1.0, RSTD[:, :], ALU.mult, ALU.mult).then_inc(nmr_ok, 1)

            dve.wait_ge(stat, 2 * NT)
            rstd(1)
            dve.wait_ge(va_init, 6)

            def norm(b):
                if not b.first:
                    dve.wait_ge(xt_ps, b.count(1))
                for t in range(TT):
                    k = b.count(TT, t)
                    ins = nc.vector.tensor_scalar(XN[:, t, :], HT[:, bass.ds(k, 1), :].rearrange("p a d -> p (a d)"),
                                                  RSTD[:, bass.ds(k, 1)], NMR[:, bass.ds(k, 1)], ALU.mult, ALU.add)
                ins.then_inc(xn_ok, 1)

            def row_max(b, par, u):
                dve.wait_ge(s_ps, b.count(SU, u + 1))
                if u % 3 == 0 and not b.first:
                    dve.wait_ge(mp_ok, (b - 1).count(G, u // 3 + 1))
                bank = BANK[S_BANK[(SU * par + u) % 2]]
                g, r = u // 3, u % 3
                if r == 0:
                    nc.vector.reduce_max(MX[:, 0, HG * g:HG * (g + 1)], bank[:, :].rearrange("p (h k) -> p h k", h=4), AX.X).then_inc(max_ok, 1)
                else:
                    nc.vector.reduce_max(MX[:, 1, HG * g + 2 * r - 2:HG * g + 2 * r], bank[:, :].rearrange("p (h k) -> p h k", h=2), AX.X).then_inc(max_ok, 1)

            def rest(b, w):
                dve.wait_ge(p0_ok, b.count(2, w + 1))
                if w == 0 and not b.first:
                    dve.wait_ge(p2_ok, b.count(1))
                for m in range(2):
                    ins = nc.vector.scalar_tensor_tensor(RES[:, 2 * w + m, :], BANK[MB][0:HALF, m * S:(m + 1) * S],
                                                         BQK[:, 2 * w + m:2 * w + m + 1], PART[0][:, 2 * w + m, :], ALU.add, ALU.subtract)
                ins.then_inc(r_ok, 1)

            def middle(b):
                dve.wait_ge(r_ok, b.count(2, 2))
                nc.vector.tensor_copy(PART[1][:, :, :], RES[:, :, :]).then_inc(p1_ok, 1)

            def values(b, par):
                dve.wait_ge(v_ps, b.count(1, 1))
                if not (b.first or b.second):
                    dve.wait_ge(av_ps, (b - 1).count(3))
                for t in range(TT):
                    ins = nc.vector.tensor_tensor(VA[par][:, t, :, 0:HS], BANK[MB][:, t * D:(t + 1) * D].rearrange("p (h d) -> p h d", h=H),
                                                  BV[:, :].rearrange("p (h d) -> p h d", h=H), ALU.add)
                ins.then_inc(v_ok, 1)

            def normalise(b, t):
                dve.wait_ge(t1_ps, b.count(2, t + 1))
                o = BANK[MA][:, 0:3 * P].rearrange("p (h c) -> p h c", h=H)
                nc.vector.reciprocal(RC[:, t, :], o[:, :, HS]).then_inc(rc_ok, 1)
                dve.wait_ge(rc_ok, b.count(2, t + 1))
                nc.vector.tensor_tensor(ON[:, t, :].rearrange("p (h c) -> p h c", h=H), o[:, :, 0:HS],
                                        RC[:, t, :].rearrange("p (h a) -> p h a", a=1).broadcast_to([P, H, HS]), ALU.mult).then_inc(on_ok, 1)

            def minus_max(b, g):
                dve.wait_ge(max_ok, b.count(SU, 3 * g + 3))
                if not b.first:
                    dve.wait_ge(mt_ps, (b - 1).count(G, g + 1))
                mx = MX[:, :, HG * g:HG * (g + 1)]
                nc.vector.tensor_scalar(MP[:, g, :, 0, :], mx, -1.0, None, ALU.mult).then_inc(mh_ok, 1)
                dve.wait_ge(mh_ok, b.count(G, g + 1))
                nc.vector.scalar_tensor_tensor(MP[:, g, :, 1, :], mx, -1.0, MP[:, g, :, 0, :], ALU.mult, ALU.subtract).then_inc(mp_ok, 1)

            def residual(b):
                dve.wait_ge(pj_ps, b.count(1, 1))
                hv = HT[:, bass.ds(b.count(TT), TT), :]
                nc.vector.tensor_tensor(H2[:, :, :], BANK[MA][:, 0:2 * D].rearrange("p (t d) -> p t d", t=2), hv, ALU.add).then_inc(h2_ok, 1)
                dve.wait_ge(h2_ok, b.count(2, 1))
                nc.vector.tensor_tensor(H2[:, :, :], H2[:, :, :], BP[:, :].rearrange("p (a d) -> p a d", a=1).broadcast_to([P, 2, D]),
                                        ALU.add).then_inc(h2_ok, 1)
                dve.wait_ge(h2_ok, b.count(2, 2))
                for t in range(TT):
                    nc.vector.bn_stats(ST2[:, t, :], H2[:, t, :]).then_inc(st2_ok, 1)
                dve.wait_ge(st2_ok, b.count(2, 2))
                nc.vector.tensor_scalar(hv, H2[:, :, :], 1.0, None, ALU.mult)
                for t in range(TT):
                    nc.vector.bn_aggr(MV2[:, t, :], ST2[:, t, :]).then_inc(mv2_ok, 1)
                dve.wait_ge(mv2_ok, b.count(2, 2))
                nc.vector.tensor_scalar(MV[:, bass.ds(b.count(TT), TT), :], MV2[:, :, :], 1.0, None, ALU.mult).then_inc(mvh_ok, 1)

            def step(b, par, has_front, has_back):
                if has_front:
                    norm(b + 1)
                row_max(b, par, 0)
                row_max(b, par, 1)
                row_max(b, par, 2)
                minus_max(b, 0)
                if has_front:
                    rest(b + 1, 0)
                row_max(b, par, 3)
                if has_front:
                    rest(b + 1, 1)
                    middle(b + 1)
                row_max(b, par, 4)
                if has_back:
                    normalise(b - 1, 0)
                row_max(b, par, 5)
                minus_max(b, 1)
                if has_back:
                    normalise(b - 1, 1)
                row_max(b, par, 6)
                row_max(b, par, 7)
                if has_front:
                    values(b + 1, 1 - par)
                row_max(b, par, 8)
                minus_max(b, 2)
                if has_back:
                    residual(b - 1)

            dve.wait_ge(nmr_ok, 1)
            norm(Image(0, 0))
            rest(Image(0, 0), 0)
            rest(Image(0, 0), 1)
            middle(Image(0, 0))
            values(Image(0, 0), 0)
            step(Image(0, 0), 0, True, False)
            with dve.Fori(0, (B - 2) // 2) as i:
                step(Image(i, 1), 1, True, True)
                step(Image(i, 2), 0, True, True)
            step(Image(0, B - 1), 1, False, True)
            normalise(Image(0, B - 1), 0)
            normalise(Image(0, B - 1), 1)
            residual(Image(0, B - 1))

            dve.wait_ge(mvh_ok, B)
            rstd(2)
            dve.wait_ge(nmr_ok, 2)
            for k in range(NT):
                if k >= 4:
                    dve.wait_ge(x2t_ps, k - 3)
                nc.vector.tensor_scalar(X2[:, k % 4, :], HT[:, k, :], RSTD[:, k:k + 1], NMR[:, k:k + 1], ALU.mult, ALU.add).then_inc(x2_ok, 1)
                if k % 8 == 7 and k > 8:
                    g = k // 8 - 1
                    dve.wait_ge(lg_ps, 8 * (g + 1))
                    nc.vector.tensor_copy(LG[:, 8 * g:8 * g + 8, :], BANK[4 + g % 2][:, 0:8 * NODES].rearrange("p (t n) -> p t n", t=8)).then_inc(lg_ok, 1)
            g = NT // 8 - 1
            dve.wait_ge(lg_ps, NT)
            nc.vector.tensor_copy(LG[:, 8 * g:8 * g + 8, :], BANK[4 + g % 2][:, 0:8 * NODES].rearrange("p (t n) -> p t n", t=8)).then_inc(lg_ok, 1)

            links = [0]

            def link(ins):
                links[0] += 1
                ins.then_inc(tree, 1)
                dve.wait_ge(tree, links[0])

            dve.wait_ge(lg_ok, NT // 8)
            nc.vector.tensor_scalar(SG[:, :, :], LG[:, :, :], 0.0, None, ALU.is_gt).then_inc(tree, 1)
            nc.vector.tensor_scalar(NS[:, :, :], LG[:, :, :], 0.0, None, ALU.is_le).then_inc(tree, 1)
            links[0] += 2
            link(nc.vector.memset(RE[:, :, 0:1], 1.0))
            for lo, hi in ((0, 1), (1, 3), (3, 7), (7, 10)):
                kids = RE[:, :, 2 * lo + 1:2 * hi + 1].rearrange("p t (n c) -> p t n c", c=2)
                nc.vector.tensor_tensor(kids[:, :, :, 0], RE[:, :, lo:hi], NS[:, :, lo:hi], ALU.mult).then_inc(tree, 1)
                links[0] += 1
                link(nc.vector.tensor_tensor(kids[:, :, :, 1], RE[:, :, lo:hi], SG[:, :, lo:hi], ALU.mult))
            link(nc.vector.reduce_sum(RE[:, :, 21:22].rearrange("p t a -> p (t a)"), RE[:, :, 15:20], AX.X))
            link(nc.vector.tensor_scalar(RE[:, :, 20:21], RE[:, :, 21:22], -1.0, 6.0, ALU.mult, ALU.add))
            dve.wait_ge(ge_ok, 1)
            nc.vector.tensor_tensor(CO[:, :, 21:32], RE[:, :, 10:21], GE[:, :, 10:21], ALU.mult).then_inc(tree, 1)
            links[0] += 1
            link(nc.vector.tensor_tensor(QQ[:, :, :], RE[:, :, 0:10], GE[:, :, 0:10], ALU.mult))
            kids = CO[:, :, 1:21].rearrange("p t (n c) -> p t n c", c=2)
            nc.vector.tensor_tensor(kids[:, :, :, 0], QQ[:, :, :], NS[:, :, 0:10], ALU.mult).then_inc(co_ok, 1)
            nc.vector.tensor_tensor(kids[:, :, :, 1], QQ[:, :, :], SG[:, :, 0:10], ALU.mult).then_inc(co_ok, 1)

            for k in range(NT // 2):
                dve.wait_ge(o_ps, k + 1)
                if k >= 4:
                    dve.wait_ge(out_ok[k // 2 % 2], 16 * (k // 4))
                nc.vector.tensor_tensor(OUTS[:, k % 4, :], BANK[4 + k % 2][:, 0:2 * D], HT[:, 2 * k:2 * k + 2, :].rearrange("p t d -> p (t d)"),
                                        ALU.add).then_inc(o_ok, 1)

        @block.tensor
        def _(pe):
            pe.wait_ge(ld_const, 16 * N_CONST)
            ja, jd = 0, 0

            def a_bank():
                if ja >= 4:
                    pe.wait_ge(act_a, ja - 3 + (1 if ja >= 20 + 4 else 0))
                return BANK[ja % 4]

            def d_bank():
                if jd >= 4:
                    pe.wait_ge(dve_d, jd - 3)
                return BANK[4 + jd % 4]

            pe.wait_ge(g2_in, 32)
            for b in range(B):
                bank = a_bank()
                for g in range(2):
                    ins = nc.tensor.transpose(bank[0:F2, g * P:(g + 1) * P], G2[:, g, b * F2:(b + 1) * F2], ID[:, :])
                ins.then_inc(pe_a, 1)
                ja += 1
            bank = a_bank()
            pe.wait_ge(act_a, 16)
            for g in range(GP):
                ins = nc.tensor.matmul(bank[0:EMB, 0:B * T2], W2S[:, g, :], G2T[:, g, :, :].rearrange("f b t -> f (b t)"), start=g == 0, stop=g == GP - 1)
            ins.then_inc(pe_a, 1)
            ja += 1
            pe.wait_ge(g1r_ok, 1)
            for q in range(4):
                bank = d_bank()
                for j in range(4):
                    ins = nc.tensor.transpose(bank[0:HALF, j * P:(j + 1) * P],
                                              G1R[:, 4 * q + j, :], ID[:, :])
                ins.then_inc(pe_d, 1)
                jd += 1
            bank = a_bank()
            pe.wait_ge(act_a, 17)
            for g in range(2):
                ins = nc.tensor.matmul(bank[:, g * D:(g + 1) * D], E2[:, g * P:(g + 1) * P], WFS[:, 2, :], start=True, stop=True)
            ins.then_inc(pe_a, 1)
            ja += 1
            nc.tensor.matmul(d_bank()[:, 0:D], BC[:, 0:1].broadcast_to([EMB, P]), WFS[:, 0, :], start=True, stop=True).then_inc(pe_d, 1)
            jd += 1
            nc.tensor.matmul(d_bank()[0:GP * F0, 0:D], W0S[:, :], WFS[:, 0, :], start=True, stop=True).then_inc(pe_d, 1)
            jd += 1
            pe.wait_ge(dve_d, 4)
            for c in range(2):
                bank = a_bank()
                for g in range(2):
                    ins = nc.tensor.matmul(bank[0:EMB, :], W1S[:, g, :], G1T[:, g, 8 * c:8 * c + 8, :].rearrange("f b t -> f (b t)"),
                                           start=g == 0, stop=g == 1)
                ins.then_inc(pe_a, 1)
                ja += 1
            pe.wait_ge(act_a, 20)
            for q in range(B // 2):
                bank = d_bank()
                for j in range(2):
                    b = 2 * q + j
                    ins = nc.tensor.matmul(bank[T1:P, j * D:(j + 1) * D], E1[:, b * T1:(b + 1) * T1], WFS[:, 1, :], start=True, stop=True)
                ins.then_inc(pe_d, 1)
                jd += 1
            for t in range(TT):
                pe.wait_ge(g0r_ok, t + 1)
                for q in range(4):
                    bank = a_bank()
                    for j in range(4):
                        b = 4 * q + j
                        ins = nc.tensor.transpose(bank[0:GP * F0, j * P:(j + 1) * P], G0R[:, t, b, :], ID[:, :])
                    ins.then_inc(pe_a, 1)
                    ja += 1
                if t == 0:
                    pe.wait_ge(ld_z2, 16 * B)
                    pe.wait_ge(ld_interp, 16)
                    pe.wait_ge(dve_d, 14)
                for q in range(B // 2):
                    bank = d_bank()
                    pe.wait_ge(act_a, 21 + 4 * t + q // 2 + 1)
                    for j in range(2):
                        b = 2 * q + j
                        ins = nc.tensor.matmul(bank[:, j * D:(j + 1) * D], LH[:, TT * b + t, :], RH[:, b, :], start=True, stop=True)
                    ins.then_inc(pe_d, 1)
                    jd += 1
            pe.wait_ge(act_a, 29)
            pe.wait_ge(dve_d, 30)

            def xn_t(b):
                pe.wait_ge(xn_ok, b.count(1, 1))
                if not (b.first or b.second):
                    pe.wait_ge(mt_ok, (b - 2).count(G, G))
                for k in range(2):
                    for t in range(TT):
                        ins = nc.tensor.transpose(BANK[MB][0:HALF, k * S + t * P:k * S + (t + 1) * P], XN[:, t, k * HALF:(k + 1) * HALF], ID[:, :])
                ins.then_inc(xt_ps, 1)

            def qk(b, w):
                pe.wait_ge(xnt_ok, b.count(1, 1))
                if w == 1:
                    pe.wait_ge(r_ok, b.count(2, 1))
                for m in range(2):
                    for k in range(2):
                        ins = nc.tensor.matmul(BANK[MB][0:HALF, m * S:(m + 1) * S], WA[:, k, (2 * w + m) * HALF:(2 * w + m + 1) * HALF],
                                               XNT[:, k, :], start=k == 0, stop=k == 1)
                ins.then_inc(qk_ps, 1)

            def v_proj(b):
                if b.first:
                    pe.wait_ge(r_ok, 2)
                else:
                    pe.wait_ge(mt_ok, (b - 1).count(G, 2))
                for t in range(TT):
                    for k in range(2):
                        ins = nc.tensor.matmul(BANK[MB][:, t * D:(t + 1) * D], XNT[:, k, t * P:(t + 1) * P], WA[:, k, 2 * D:3 * D],
                                               start=k == 0, stop=k == 1)
                ins.then_inc(v_ps, 1)

            def scores(b, par, u):
                n = SU * par + u
                if b.first:
                    if u >= 2:
                        pe.wait_ge(max_ok, u - 1)
                else:
                    pe.wait_ge(max_ok, b.count(SU, u - 1))
                bank = BANK[S_BANK[n % 2]]
                g, r = u // 3, u % 3
                if r == 0:
                    for j in range(HG):
                        h = HG * g + j
                        nc.tensor.matmul(bank[:, j * P:(j + 1) * P], QS[par][0:KQ, h, 0:P], KS[par][0:KQ, h, 0:P], start=j == 0, stop=False)
                    nc.tensor.matmul(bank[:, :], IDB[:, :], MASKQ[:, :, :].rearrange("p a k -> p (a k)"), start=False, stop=True).then_inc(s_ps, 1)
                else:
                    for j in range(2):
                        h = HG * g + 2 * (r - 1) + j
                        nc.tensor.matmul(bank[:, j * S:(j + 1) * S], QS[par][0:KQ, h, P:S], KS[par][0:KQ, h, :], start=j == 0, stop=False)
                    nc.tensor.matmul(bank[:, :].rearrange("p (h k) -> p h k", h=2)[:, :, P:S], IDB[:, :], MASKQ[:, 0:2, :],
                                     start=False, stop=True).then_inc(s_ps, 1)

            def max_t(b, g):
                pe.wait_ge(mp_ok, b.count(G, g + 1))
                bank = MA if g == 0 else MB
                if g == 0 and not (b.first or b.second):
                    pe.wait_ge(h2_ok, (b - 1).count(2))
                if g == 1 and not b.last:
                    pe.wait_ge(r_ok, b.count(2, 4))
                if g == 2 and not b.last:
                    pe.wait_ge(v_ok, b.count(1, 2))
                if g > 0 and b.last:
                    pe.wait_ge(mt_ok, b.count(G, 0 if g == 1 else 2))
                for t in range(TT):
                    ins = nc.tensor.transpose(BANK[bank][0:2 * HG, t * P // 2:(t + 1) * P // 2].bitcast(bf16),
                                              MP[:, g, t, :, :].rearrange("p a h -> p (a h)"), IDB[:, :])
                ins.then_inc(mt_ps, 1)

            def scores_t(b, par, v):
                if b.first:
                    if v >= 2:
                        pe.wait_ge(exp_ok, v - 1)
                else:
                    pe.wait_ge(exp_ok, b.count(SU, v - 1))
                bank = BANK[T_BANK[(SU * par + v) % 2]]
                g, r = v // 3, v % 3
                if r == 0:
                    pe.wait_ge(m_in, b.count(G * 32, 32 * (g + 1)))
                if r < 2:
                    for j in range(2):
                        h = HG * g + 2 * r + j
                        ins = nc.tensor.matmul(bank[:, j * S:(j + 1) * S], KS[par][:, h, 0:P], QS[par][:, h, :], start=j == 0, stop=j == 1)
                else:
                    for j in range(HG):
                        h = HG * g + j
                        ins = nc.tensor.matmul(bank[:, j * P:(j + 1) * P], KS[par][:, h, P:S], QS[par][:, h, P:S], start=j == 0, stop=j == HG - 1)
                ins.then_inc(st_ps, 1)

            def weighted(b, par, g):
                pe.wait_ge(cut_ok, b.count(SU, 3 * g + 3))
                if g == 0 and not b.first:
                    pe.wait_ge(ot_ok, (b - 1).count(2, 1))
                if g == 2 and not b.first:
                    pe.wait_ge(ot_ok, b.count(2))
                if g == 0:
                    pe.wait_ge(v_ok, b.count(1, 1))
                bank = BANK[O_BANK[g // 2]]
                c = (g % 2) * S
                for j in range(4):
                    nc.tensor.matmul(bank[32 * j:32 * j + 32, c:c + S], VA[par][:, 0, 4 * g + j, :],
                                     PT[:, 3 * g + j // 2, (j % 2) * S:(j % 2 + 1) * S], start=True, stop=False, skip_group_check=True)
                for j in range(4):
                    ins = nc.tensor.matmul(bank[32 * j:32 * j + 32, c + P:c + S], VA[par][:, 1, 4 * g + j, :],
                                           PT[:, 3 * g + 2, j * P:(j + 1) * P], start=False, stop=True, skip_group_check=True)
                ins.then_inc(av_ps, 1)

            def out_t(b, t):
                pe.wait_ge(ot_ok, b.count(2, 2))
                if t == 1:
                    pe.wait_ge(on_ok, b.count(2, 1))
                elif b.last:
                    pe.wait_ge(h2_ok, b.count(2))
                else:
                    pe.wait_ge(mt_ok, b.count(G, G + 1))
                for g in range(3):
                    ins = nc.tensor.transpose(BANK[MA][:, g * P:(g + 1) * P], OT[:, g, t * P:(t + 1) * P], ID[:, :])
                ins.then_inc(t1_ps, 1)

            def on_t(b):
                pe.wait_ge(on_ok, b.count(2, 2))
                for k in range(2):
                    for t in range(TT):
                        ins = nc.tensor.transpose(BANK[MA][0:HALF, k * S + t * P:k * S + (t + 1) * P], ON[:, t, k * HALF:(k + 1) * HALF], ID[:, :])
                ins.then_inc(t2_ps, 1)

            def project(b):
                pe.wait_ge(ont_ok, b.count(1, 1))
                for t in range(TT):
                    for k in range(2):
                        ins = nc.tensor.matmul(BANK[MA][:, t * D:(t + 1) * D], ONT[:, k, t * P:(t + 1) * P], WP[:, k, :], start=k == 0, stop=k == 1)
                ins.then_inc(pj_ps, 1)

            def step(b, par, has_front, has_back):
                pe.wait_ge(stacked, b.count(6 * 16, 6 * 16))
                scores(b, par, 0)
                scores(b, par, 1)
                if has_front:
                    xn_t(b + 1)
                if has_back:
                    weighted(b - 1, 1 - par, 1)
                scores(b, par, 2)
                if has_front:
                    qk(b + 1, 0)
                if has_back:
                    for v in range(6, 9):
                        scores_t(b - 1, 1 - par, v)
                max_t(b, 0)
                if has_front:
                    qk(b + 1, 1)
                if has_back:
                    weighted(b - 1, 1 - par, 2)
                scores(b, par, 3)
                scores(b, par, 4)
                if has_back:
                    out_t(b - 1, 0)
                scores(b, par, 5)
                for v in range(2):
                    scores_t(b, par, v)
                if has_back:
                    out_t(b - 1, 1)
                scores_t(b, par, 2)
                max_t(b, 1)
                if has_back:
                    on_t(b - 1)
                scores(b, par, 6)
                scores(b, par, 7)
                if has_front:
                    v_proj(b + 1)
                scores(b, par, 8)
                if has_back:
                    project(b - 1)
                for v in range(3, 6):
                    scores_t(b, par, v)
                weighted(b, par, 0)
                max_t(b, 2)

            xn_t(Image(0, 0))
            qk(Image(0, 0), 0)
            qk(Image(0, 0), 1)
            v_proj(Image(0, 0))
            pe.wait_ge(v_ok, 1)
            step(Image(0, 0), 0, True, False)
            with pe.Fori(0, (B - 2) // 2) as i:
                step(Image(i, 1), 1, True, True)
                step(Image(i, 2), 0, True, True)
            step(Image(0, B - 1), 1, False, True)
            last = Image(0, B - 1)
            weighted(last, 1, 1)
            for v in range(6, 9):
                scores_t(last, 1, v)
            weighted(last, 1, 2)
            out_t(last, 0)
            out_t(last, 1)
            on_t(last)
            project(last)

            def logits(k):
                pe.wait_ge(x2t_ok, k + 1)
                if k % 8 == 0 and k >= 16:
                    pe.wait_ge(lg_ok, k // 8 - 1)
                for c in range(2):
                    ins = nc.tensor.matmul(BANK[4 + (k // 8) % 2][:, (k % 8) * NODES:(k % 8 + 1) * NODES], X2T[k % 4][:, c, :], WIN[:, c, :],
                                           start=c == 0, stop=c == 1)
                ins.then_inc(lg_ps, 1)

            for k in range(NT):
                pe.wait_ge(x2_ok, k + 1)
                if k >= 2:
                    pe.wait_ge(x2t_ok, k - 1)
                for c in range(2):
                    ins = nc.tensor.transpose(BANK[k % 2][0:HALF, c * P:(c + 1) * P], X2[:, k % 4, c * HALF:(c + 1) * HALF], ID[:, :])
                ins.then_inc(x2t_ps, 1)
                if k >= 1:
                    logits(k - 1)
            logits(NT - 1)

            def output(k):
                pe.wait_ge(cot_ok, k + 1)
                if k % 2 == 0 and k >= 4:
                    pe.wait_ge(o_ok, k // 2 - 1)
                ins = nc.tensor.matmul(BANK[4 + (k // 2) % 2][:, (k % 2) * D:(k % 2 + 1) * D], COT[k % 4][:, :], WEX[:, :], start=True, stop=True)
                if k % 2:
                    ins.then_inc(o_ps, 1)

            pe.wait_ge(co_ok, 2)
            pe.wait_ge(lg_ok, NT // 8)
            pe.wait_ge(va_init, 8)
            for k in range(NT):
                if k >= 2:
                    pe.wait_ge(cot_ok, k - 1)
                nc.tensor.transpose(BANK[k % 2][0:NCO, 0:P], CO[:, k, :], ID[:, :]).then_inc(cot_ps, 1)
                if k >= 1:
                    output(k - 1)
            output(NT - 1)


def _interp(length):
    import numpy as np
    pos = np.clip((np.arange(S, dtype=np.float32) + np.float32(0.5)) * np.float32(length / S) - np.float32(0.5), 0, length - 1)
    lo = np.floor(pos).astype(np.int32)
    hi = np.minimum(lo + 1, length - 1)
    w = (pos - lo).astype(np.float32)
    m = np.zeros((length, S), np.float32)
    np.add.at(m, (lo, np.arange(S)), np.float32(1) - w)
    np.add.at(m, (hi, np.arange(S)), w)
    return m


def kernel(x, L0_tok_W0, L0_tok_b0, L0_tok_W1, L0_tok_b1, L0_tok_W2, L0_tok_b2, L0_tok_Wf, L0_tok_bf,
           L0_tok_idx0, L0_tok_idx1, L0_tok_idx2, L0_attn_W_attn, L0_attn_b_attn, L0_attn_W_proj, L0_attn_b_proj,
           L0_ffn_weights_in, L0_ffn_weights_out):
    import numpy as np
    import concourse.bacc as bacc
    from concourse.bass_utils import run_bass_kernel_spmd

    x = np.asarray(x)

    def patches(p):
        h = IMG // p
        t = x.reshape(B, CH, h, p, h, p).transpose(2, 4, 0, 3, 5, 1)
        return t.reshape(h * h, B * p * p * CH)

    def by_width(a):
        return a.reshape(a.shape[:-1] + (2, H, HS)).swapaxes(-1, -2).reshape(a.shape)

    w_attn, b_attn = np.asarray(L0_attn_W_attn), np.asarray(L0_attn_b_attn)
    i0, i1, i2 = (np.asarray(i) for i in (L0_tok_idx0, L0_tok_idx1, L0_tok_idx2))
    wout = np.asarray(L0_ffn_weights_out)
    bf16 = mybir.dt.np(mybir.dt.bfloat16)
    tri = np.tril(np.ones((P, P), bool))
    masked = np.float32(-2.0 ** 126)
    arrays = {
        "x0": patches(1), "x1": patches(2), "x2": patches(4),
        "ix0": i0.reshape(TT, P, GP).transpose(1, 0, 2).reshape(P, TT * GP),
        "ix1": i1.reshape(T1, 2, GP // 2).transpose(1, 0, 2).reshape(P, GP // 2),
        "ix2": i2.reshape(T2, 2, GP // 2).transpose(2, 0, 1).reshape(P, 2),
        "w0": np.asarray(L0_tok_W0), "w1t": np.asarray(L0_tok_W1).T, "w2t": np.asarray(L0_tok_W2).T,
        "wft": np.asarray(L0_tok_Wf).T, "bcol": np.stack([np.asarray(v) for v in (L0_tok_b0, L0_tok_b1, L0_tok_b2)], 1),
        "bf": np.asarray(L0_tok_bf),
        "wa": np.concatenate([by_width(w_attn[:, :2 * D]), w_attn[:, 2 * D:]], 1), "bqk": by_width(b_attn[:2 * D]).reshape(4, HALF).T,
        "bv": b_attn[2 * D:],
        "wp": np.asarray(L0_attn_W_proj), "bp": np.asarray(L0_attn_b_proj),
        "wint": np.asarray(L0_ffn_weights_in).T,
        "wext": wout[np.array(list(range(NODES)) + [NODES - 1] * (NCO - NODES))],
        "identf": np.eye(P, dtype=np.float32), "identb": np.eye(P, dtype=np.float32).astype(bf16),
        "maskq": np.where(tri, np.float32(0), masked).astype(bf16),
        "interp": np.concatenate([_interp(T2), _interp(T1)]),
    }
    arrays = {n: np.ascontiguousarray(a) for n, a in arrays.items()}
    nc = bacc.Bacc("TRN2", target_bir_lowering=False, num_devices=1)
    args = [nc.dram_tensor(n, a.shape, mybir.dt.from_np(a.dtype), kind="ExternalInput").ap() for n, a in arrays.items()]
    out = nc.dram_tensor("out", (B * S, D), mybir.dt.float32, kind="ExternalOutput").ap()
    parts = nc.dram_tensor("parts", (B, PARTS, 4, HALF, S), mybir.dt.bfloat16, kind="Internal").ap()
    vit_tower_kernel(nc, *args, out, parts)
    r = run_bass_kernel_spmd(nc, [arrays], core_ids=[0])
    return r.results[0]["out"].reshape(B, S, D)
```

```python
import concourse.bass as bass
from concourse import mybir
from contextlib import ExitStack

B, CH, IMG = 16, 3, 64
GP, EMB = 16, 64
D = 3 * EMB
S = IMG * IMG // GP
P = 128
TT = S // P
NT = B * TT
H, HS = 12, 16
HALF = D // 2
F0, F1, F2 = CH, 4 * CH, 16 * CH
T1, T2 = S // 4, S // 16
NODES = 21
NP = 32
QD = 4
NQ = NT // QD
XQ = 4
NH = NT // 2
KO = 6 * NODES
EPS = 1e-5
PARTS = 3
KQ = 6 * HS
KM = KQ + 2
G = 3
HG = H // G
SU = 9
SCALE = 0.25


class Image:

    def __init__(self, pair, off):
        self.pair, self.off = pair, off
        number = off if isinstance(pair, int) else None
        self.first, self.second, self.late, self.last = number == 0, number == 1, number == B - 2, number == B - 1

    def __add__(self, n):
        return Image(self.pair, self.off + n)

    def __sub__(self, n):
        return Image(self.pair, self.off - n)

    def count(self, per, more=0):
        return self.pair * (2 * per) + (self.off * per + more)


def vit_tower_kernel(nc, x0, x1, x2, ix0, ix1, ix2, w0, w1t, w2t, wft, bcol, bf,
                     wa, bqk, bv, wp, bp, wint, wext, sel, identf, identb, maskq, interp,
                     out, parts):
    fp32, bf16, i32 = mybir.dt.float32, mybir.dt.bfloat16, mybir.dt.int32
    ALU = mybir.AluOpType
    ACT = mybir.ActivationFunctionType
    AX = mybir.AxisListType

    ctx = ExitStack()
    with ctx:
        def sb(name, shape, dt=fp32):
            return ctx.enter_context(nc.sbuf_tensor(name, shape, dt))

        def sem(name):
            return ctx.enter_context(nc.semaphore(name))

        ID = sb("ID", [P, P])
        CARRY = sb("CARRY", [1, 2])
        IDB = sb("IDB", [P, P], bf16)
        MASKQ = sb("MASKQ", [P, 4, P], bf16)
        W0S = sb("W0S", [EMB, GP * F0])
        W1S = sb("W1S", [HALF, 2, EMB])
        W2S = sb("W2S", [2 * F2, GP // 2, EMB])
        WFS = sb("WFS", [EMB, 3, D])
        WA = sb("WA", [HALF, 2, 3 * D])
        WP = sb("WP", [HALF, 2, D])
        WIN = sb("WIN", [HALF, 2, NP])
        SEL = sb("SEL", [KO, PARTS])
        W6 = sb("W6", [KO, D], bf16)
        BC = sb("BC", [EMB, 3])
        BFB = sb("BFB", [P, D])
        BQK = sb("BQK", [HALF, 4])
        BV = sb("BV", [P, D])
        BP = sb("BP", [P, D])

        I0 = sb("I0", [P, TT * GP], i32)
        I1 = sb("I1", [P, GP // 2], i32)
        I2 = sb("I2", [P, 2], i32)
        CB = sb("CB", [P, D])
        C0 = sb("C0", [GP * F0, D])
        HT = sb("HT", [P, NT, D])
        ST = sb("ST", [P, NT, 6])
        MV = sb("MV", [P, NT, 2])
        VE = sb("VE", [P, NT])
        SD = sb("SD", [P, NT])
        RSTD = sb("RSTD", [P, NT])
        NMR = sb("NMR", [P, NT])

        XN = sb("XN", [P, TT, D])
        XNT = sb("XNT", [HALF, 2, S])
        PART = [sb(f"PART{i}", [HALF, 4, S], bf16) for i in range(PARTS)]
        RES = sb("RES", [HALF, 4, S])
        QS = [sb(f"QS{i}", [KM, H, S], bf16) for i in range(2)]
        KS = [sb(f"KS{i}", [KM, H, S], bf16) for i in range(2)]
        VA = [sb(f"VA{i}", [P, TT, H, 32]) for i in range(2)]
        MX = sb("MX", [P, TT, H])
        MP = sb("MP", [P, G, TT, 2, HG], bf16)
        MT = sb("MT", [2 * HG, G, S], bf16)
        OT = sb("OT", [P, 3, S])
        RC = sb("RC", [P, TT, H])
        ON = sb("ON", [P, TT, D])
        ONT = sb("ONT", [HALF, 2, S])
        H2 = sb("H2", [P, TT, D])
        MV2 = sb("MV2", [P, TT, 2])
        ST2 = sb("ST2", [P, TT, 6])

        with ExitStack() as early:
            tok = lambda name, shape, dt=fp32: early.enter_context(nc.sbuf_tensor(name, shape, dt))
            G0 = tok("G0", [P, TT, GP, B * F0])
            G1 = tok("G1", [P, GP // 2, B * F1])
            G2 = tok("G2", [P, 2, B * F2])
            G0R = tok("G0R", [P, TT, B, GP * F0])
            G1R = tok("G1R", [P, B, HALF])
            G1T = tok("G1T", [HALF, 2, B, T1])
            G2R = tok("G2R", [P, B, 2 * F2])
            G2T = tok("G2T", [2 * F2, GP // 2, B, T2])
            E1 = tok("E1", [EMB, B * T1])
            E2 = tok("E2", [EMB, B * T2])
            Z2 = tok("Z2", [P, 2, D])
            LH = tok("LH", [P, NT, P])
            RH = tok("RH", [P, B, D])

        WEX, WR = H2[0:KO, 0, :], H2[0:KO, 1, :]
        WPART = ON[0:KO, :, :].rearrange("p t d -> p (t d)").bitcast(bf16)[:, 0:PARTS * D].rearrange("p (n d) -> p n d", n=PARTS)
        PT = sb("PT", [P, SU, 512])

        X2 = sb("X2", [P, XQ * QD, D])
        X2T = [sb(f"X2T{i}", [HALF, 2, QD * P]) for i in range(2)]
        LGT = sb("LGT", [P, P])
        LG = sb("LG", [P, NT, NP])
        GE = sb("GE", [P, NT, NODES])
        SG = sb("SG", [P, NT, NODES])
        NS = sb("NS", [P, NT, NODES])
        RE = sb("RE", [P, NT, 22])
        QQ = sb("QQ", [P, NT, 10])
        QE = sb("QE", [P, NT, 12])
        CO = sb("CO", [P, NT, NODES])
        CR = sb("CR", [P, NT, NODES])
        C6 = sb("C6", [P, NT, KO], bf16)
        COT = [sb(f"COT{i}", [KO, QD * P], bf16) for i in range(2)]

        BANK = [ctx.enter_context(nc.psum_tensor(f"bank{i}", [P, 512], fp32)) for i in range(8)]

        ld_first = sem("ld_first")
        g2r_ok = sem("g2r_ok")
        ht_ps, ht_ok = sem("ht_ps"), sem("ht_ok")
        ld_idx, ld_const, ld_interp, ld_z2 = sem("ld_idx"), sem("ld_const"), sem("ld_interp"), sem("ld_z2")
        g2_in, g1_in = sem("g2_in"), sem("g1_in")
        g1r_ok, g0r_ok = sem("g1r_ok"), sem("g0r_ok")
        g0_in = [sem(f"g0_in{t}") for t in range(TT)]
        pe_a, pe_d = sem("pe_a"), sem("pe_d")
        act_a, dve_d = sem("act_a"), sem("dve_d")
        va_init = sem("va_init")
        stat, var_ok, sd_ok, rstd_ok, nmr_ok = sem("stat"), sem("var_ok"), sem("sd_ok"), sem("rstd_ok"), sem("nmr_ok")
        xn_ok, xt_ps, xnt_ok, qk_ps, p0_ok, r_ok, p1_ok, p2_ok = [
            sem(n) for n in ("xn_ok", "xt_ps", "xnt_ok", "qk_ps", "p0_ok", "r_ok", "p1_ok", "p2_ok")]
        stored, stacked = [sem(f"stored_{w}") for w in "qk"], sem("stacked")
        v_ps, v_ok = sem("v_ps"), sem("v_ok")
        s_ps, max_ok, mh_ok, mp_ok, mt_ps, mt_ok = [
            sem(n) for n in ("s_ps", "max_ok", "mh_ok", "mp_ok", "mt_ps", "mt_ok")]
        st_ps, exp_ok, av_ps, ot_ok, m_in, cut_ok, carried = [sem(n) for n in ("st_ps", "exp_ok", "av_ps", "ot_ok", "m_in", "cut_ok", "carried")]
        t1_ps, rc_ok, on_ok, t2_ps, ont_ok, pj_ps, h2_ok = [
            sem(n) for n in ("t1_ps", "rc_ok", "on_ok", "t2_ps", "ont_ok", "pj_ps", "h2_ok")]
        w6_ok, x2p_ok, lgt_ok, lt_ps, ch_ok, cr_ok, cm_ok, c6_ok = [
            sem(n) for n in ("w6_ok", "x2p_ok", "lgt_ok", "lt_ps", "ch_ok", "cr_ok", "cm_ok", "c6_ok")]
        st2_ok, mv2_ok, mvh_ok = sem("st2_ok"), sem("mv2_ok"), sem("mvh_ok")
        x2_ok, x2t_ps, x2t_ok, lg_ps, lg_ok, ge_ok, tree = [
            sem(n) for n in ("x2_ok", "x2t_ps", "x2t_ok", "lg_ps", "lg_ok", "ge_ok", "tree")]
        co_ok, cot_ps, cot_ok, o_ps, o_ok = [
            sem(n) for n in ("co_ok", "cot_ps", "cot_ok", "o_ps", "o_ok")]
        out_ok = sem("out_ok")

        N_FIRST, N_CONST = 7, 11
        S_BANK = [0, 1]
        T_BANK = [2, 3]
        O_BANK = [4, 5]
        MA, MB = 6, 7
        OUT_BANK = [2, 3, 6, 7]
        H_BANK = [4, 5, 6]
        EVEN, SECOND, ODD = slice(0, NT, 2), slice(1, 4, 2), slice(5, NT, 2)

        def pair(k):
            return 2 * ((k + 1) % 2) if k else 0

        T1_BANK = [MA, O_BANK[1]]

        block = ctx.enter_context(nc.Block())

        @block.sync
        def _(sp):
            for t, src in ((I2, ix2), (I1, ix1), (I0, ix0)):
                sp.dma_start(t[:, :], src).then_inc(ld_idx, 16)
            sp.dma_start(ID[:, :], identf).then_inc(ld_first, 16)
            for h in range(2):
                sp.dma_start(W2S[h * F2:(h + 1) * F2, :, :],
                             w2t[h * GP // 2 * F2:(h + 1) * GP // 2 * F2, :].rearrange("(g f) e -> f g e", g=GP // 2)).then_inc(ld_first, 16)
            sp.dma_start(W1S[:, :, :], w1t.rearrange("(g f) e -> f g e", g=2)).then_inc(ld_first, 16)
            sp.dma_start(WFS[:, :, :], wft.rearrange("(l e) o -> e l o", l=3)).then_inc(ld_first, 16)
            sp.dma_start(W0S[:, :], w0).then_inc(ld_first, 16)
            sp.dma_start(BC[:, :], bcol).then_inc(ld_first, 16)
            for t, src in ((BFB, bf), (BV, bv), (BP, bp)):
                sp.dma_start(t[:, :], src.rearrange("(a n) -> a n", a=1).broadcast_to([P, D])).then_inc(ld_const, 16)
            sp.dma_start(LH[GP * F0:P, :, :].rearrange("k (b t) n -> k b (t n)", b=B),
                         interp.rearrange("k (a n) -> k a n", a=1).broadcast_to([T2 + T1, B, S])).then_inc(ld_interp, 16)
            sp.dma_start(BQK[:, :], bqk).then_inc(ld_const, 16)
            sp.dma_start(WA[:, :, :], wa.rearrange("(k p) n -> p k n", k=2)).then_inc(ld_const, 16)
            sp.dma_start(WP[:, :, :], wp.rearrange("(k p) n -> p k n", k=2)).then_inc(ld_const, 16)
            sp.dma_start(WIN[:, :, :], wint.rearrange("(k p) n -> p k n", k=2)).then_inc(ld_const, 16)
            sp.dma_start(WEX, wext).then_inc(ld_const, 16)
            sp.dma_start(SEL[:, :], sel).then_inc(ld_const, 16)
            sp.dma_start(IDB[:, :], identb).then_inc(ld_const, 16)
            sp.dma_start(MASKQ[:, :, :], maskq.rearrange("q (a k) -> q a k", a=1).broadcast_to([P, 4, P])).then_inc(ld_const, 16)
            sp.wait_ge(act_a, 6)
            for b in range(B):
                r = (b % 8) * T2
                sp.dma_start(RH[GP * F0:GP * F0 + T2, b, :], Z2[r:r + T2, b // 8, :]).then_inc(ld_z2, 16)

            def step(b, par, has_front, has_own=True):
                def fixed(value):
                    return value if isinstance(value, int) else sp.snap(value)

                f = b + 1
                image, half, whole = fixed(f.count(1)), fixed(f.count(2, 1)), fixed(f.count(2, 2))
                in_dram = fixed(f.count(16 * PARTS, 16 * PARTS))
                in_rows = [fixed(b.count(G, g + 1)) for g in range(G)] if has_own else None
                view = parts[bass.ds(image, 1), :, :, :, :].rearrange("a n (w m) p s -> (a n) w (m p s)", w=2) if has_front else None

                def store(w, n):
                    if has_front:
                        sp.wait_ge((p0_ok, p1_ok, p2_ok)[n], half if w == 0 else whole)
                        sp.dma_start(parts[bass.ds(image, 1), n, 2 * w:2 * w + 2, :, :].rearrange("a m p s -> p (a m) s"),
                                     PART[n][:, 2 * w:2 * w + 2, :]).then_inc(stored[w], 16)

                def load(w, dst):
                    if has_front:
                        sp.wait_ge(stored[w], in_dram)
                        row = 0
                        for n in (3, 2, 1):
                            src = view[0:n, w, :] if w else view[3 - n:4 - n, w, :].broadcast_to([n, H * HS * S])
                            sp.dma_start(dst[row:row + n * HS, :, :].rearrange("r h s -> r (h s)"),
                                         src.rearrange("n (d c) -> n d c", d=HS)).then_inc(stacked, 16)
                            row += n * HS

                def maxima(g):
                    if has_own:
                        sp.wait_ge(mt_ok, in_rows[g])
                        sp.dma_start(QS[par][KQ:KM, HG * g:HG * (g + 1), :],
                                     MT[:, g, :]).then_inc(m_in, 16)

                store(0, 0)
                store(0, 1)
                maxima(0)
                store(0, 2)
                store(1, 0)
                store(1, 1)
                store(1, 2)
                maxima(1)
                load(0, QS[1 - par])
                load(1, KS[1 - par])
                maxima(2)

            step(Image(0, -1), 1, True, False)
            step(Image(0, 0), 0, True)
            step(Image(0, 1), 1, True)
            with sp.Fori(1, B // 2 - 1) as i:
                step(Image(i, 0), 0, True)
                step(Image(i, 1), 1, True)
            step(Image(0, B - 2), 0, True)
            step(Image(0, B - 1), 1, False)

            for k in range(NQ):
                sp.wait_ge(o_ok, 2 * k + 2)
                sp.dma_start(out[QD * k * P:QD * (k + 1) * P, :].rearrange("(t p) d -> p t d", p=P),
                             HT[:, QD * k:QD * (k + 1), :]).then_inc(out_ok, 16)
            sp.wait_ge(out_ok, 16 * NQ)

        @block.gpsimd
        def _(pool):
            pool.wait_ge(ld_idx, 48)
            for j in range(2):
                pool.indirect_dma_start(G2[:, j, :], None, x2, bass.IndirectOffsetOnAxis(ap=I2[:, j:j + 1], axis=0)).then_inc(g2_in, 16)
            for j in range(GP // 2):
                pool.indirect_dma_start(G1[:, j, :], None, x1, bass.IndirectOffsetOnAxis(ap=I1[:, j:j + 1], axis=0)).then_inc(g1_in, 16)
            for t in range(TT):
                for g in range(GP):
                    j = t * GP + g
                    pool.indirect_dma_start(G0[:, t, g, :], None, x0, bass.IndirectOffsetOnAxis(ap=I0[:, j:j + 1], axis=0)).then_inc(g0_in[t], 16)
            for i in range(2):
                pool.memset(VA[i][:, :, :, HS:32], 0.0).then_inc(va_init, 1)
            pool.wait_ge(va_init, 2)
            for i in range(2):
                pool.memset(VA[i][:, :, :, HS:HS + 1], 1.0).then_inc(va_init, 1)
                pool.wait_ge(va_init, 3 + 2 * i)
                pool.memset(KS[i][KQ:KM, :, :], 1.0).then_inc(va_init, 1)
                pool.wait_ge(va_init, 4 + 2 * i)
            pool.memset(CARRY[:, :], 0.0).then_inc(va_init, 1)
            pool.wait_ge(va_init, 7)

            def low(b, w):
                pool.wait_ge(p1_ok, b.count(2, w + 1))
                pool.tensor_tensor(PART[2][:, 2 * w:2 * w + 2, :], RES[:, 2 * w:2 * w + 2, :], PART[1][:, 2 * w:2 * w + 2, :],
                                   ALU.subtract).then_inc(p2_ok, 1)

            def causal(b, g, own):
                n = 2 * g + own
                if not (b.first and n == 0):
                    pool.wait_ge(carried, b.count(6, n))
                pool.wait_ge(exp_ok, b.count(SU, 3 * g + 2 + own))
                pool.tensor_tensor(CARRY[:, 1:2], CARRY[:, 0:1], CARRY[:, 0:1], ALU.add).then_inc(carried, 1)
                for r in ([0, 1], [2])[own]:
                    n = 2 if r < 2 else 4
                    e = PT[:, 3 * g + r, :].rearrange("p (h q) -> p h q", h=n)[:, :, 0:P]
                    pool.affine_select(out=e, in_=e, compare_op=ALU.is_ge, fill=0.0, base=0,
                                       pattern=[[0, n], [1, P]], channel_multiplier=-1).then_inc(cut_ok, 1)

            def step(b, has_front, has_back):
                if has_back:
                    causal(b - 1, 2, 0)
                if has_front:
                    low(b + 1, 0)
                if has_back:
                    causal(b - 1, 2, 1)
                if has_front:
                    low(b + 1, 1)
                for g in range(2):
                    causal(b, g, 0)
                    causal(b, g, 1)

            low(Image(0, 0), 0)
            low(Image(0, 0), 1)
            step(Image(0, 0), True, False)
            step(Image(0, 1), True, True)
            with pool.Fori(1, B // 2 - 1) as i:
                step(Image(i, 0), True, True)
                step(Image(i, 1), True, True)
            step(Image(0, B - 2), True, True)
            step(Image(0, B - 1), False, True)
            causal(Image(0, B - 1), 2, 0)
            causal(Image(0, B - 1), 2, 1)

            for k in range(2, NQ):
                pool.wait_ge(nmr_ok, 4 if k < NQ - 1 else 5)
                if k >= XQ:
                    pool.wait_ge(x2t_ps, k - XQ + 1)
                for j in range(QD * k + 2, QD * k + 4):
                    ins = nc.gpsimd.tensor_scalar(X2[:, j % (XQ * QD), :], HT[:, j, :], RSTD[:, j:j + 1], NMR[:, j:j + 1], ALU.mult, ALU.add)
                ins.then_inc(x2p_ok, 1)

            pool.wait_ge(ch_ok, 1)
            nc.gpsimd.tensor_tensor(CR[:, 0:NH, :], CO[:, 0:NH, :], C6[:, 0:NH, 0:NODES], ALU.subtract).then_inc(cr_ok, 1)
            pool.wait_ge(cm_ok, 1)
            nc.gpsimd.tensor_tensor(C6[:, 0:NH, 5 * NODES:], CR[:, 0:NH, :], C6[:, 0:NH, 3 * NODES:4 * NODES], ALU.subtract).then_inc(c6_ok, 1)

        @block.scalar
        def _(act):
            act.wait_ge(ld_first, 16 * N_FIRST)
            job = 0

            def a_bank():
                return BANK[job % 4]

            for q in range(4):
                act.wait_ge(pe_a, job + 1)
                nc.scalar.copy(G2T[:, :, :, :].rearrange("f g b t -> f b g t")[:, 4 * q:4 * q + 4, :, :],
                               a_bank()[0:2 * F2, :].rearrange("f (b g t) -> f b g t", b=4, t=T2)).then_inc(act_a, 1)
                job += 1
            act.wait_ge(pe_a, job + 1)
            nc.scalar.activation(E2[:, :], a_bank()[0:EMB, 0:B * T2], ACT.Identity, bias=BC[:, 2:3]).then_inc(act_a, 1)
            job += 1
            act.wait_ge(pe_a, job + 1)
            nc.scalar.copy(Z2[:, :, :], a_bank()[:, 0:2 * D].rearrange("p (a d) -> p a d", a=2)).then_inc(act_a, 1)
            job += 1
            act.wait_ge(dve_d, 6)
            nc.scalar.copy(RH[0:GP * F0, :, :], C0[:, :].rearrange("p (a d) -> p a d", a=1).broadcast_to([GP * F0, B, D])).then_inc(act_a, 1)
            for c in range(2):
                act.wait_ge(pe_a, job + 1)
                nc.scalar.activation(E1[:, c * 512:(c + 1) * 512], a_bank()[0:EMB, :], ACT.Identity, bias=BC[:, 1:2]).then_inc(act_a, 1)
                job += 1

            def patches_t(t, q):
                n = 4 * t + q
                act.wait_ge(pe_a, job + n + 1)
                nc.scalar.copy(LH[0:GP * F0, :, :].rearrange("k (b t) n -> k b t n", t=TT)[:, 4 * q:4 * q + 4, t, :],
                               BANK[(job + n) % 4][0:GP * F0, :].rearrange("k (b n) -> k b n", b=4)).then_inc(act_a, 1)

            def tokens(t, q):
                n = B // 2 * t + q
                act.wait_ge(ht_ps, n + 1)
                nc.scalar.copy(HT[:, :, :].rearrange("p (b t) d -> p b t d", t=TT)[:, 2 * q:2 * q + 2, t, :],
                               BANK[H_BANK[n % 3]][:, 0:2 * D].rearrange("p (b d) -> p b d", b=2)).then_inc(ht_ok, 1)

            def deviations(round_, tiles):
                act.wait_ge(var_ok, round_)
                nc.scalar.activation(SD[:, tiles], VE[:, tiles], ACT.Sqrt).then_inc(sd_ok, 1)

            def front(b):
                act.wait_ge(xt_ps, b.count(1, 1))
                nc.scalar.copy(XNT[:, :, :], BANK[MB][0:HALF, :].rearrange("p (k s) -> p k s", k=2)).then_inc(xnt_ok, 1)

            def first_part(b, w):
                act.wait_ge(qk_ps, b.count(2, w + 1))
                if not b.first:
                    act.wait_ge(stored[w], b.count(16 * PARTS))
                for m in range(2):
                    ins = nc.scalar.activation(PART[0][:, 2 * w + m, :], BANK[MB][0:HALF, m * S:(m + 1) * S],
                                               ACT.Identity, bias=BQK[:, 2 * w + m:2 * w + m + 1])
                ins.then_inc(p0_ok, 1)

            def middle(b, w):
                act.wait_ge(r_ok, b.count(2, w + 1))
                nc.scalar.copy(PART[1][:, 2 * w:2 * w + 2, :], RES[:, 2 * w:2 * w + 2, :]).then_inc(p1_ok, 1)

            def outputs_t(b):
                act.wait_ge(t2_ps, b.count(1, 1))
                nc.scalar.copy(ONT[:, :, :], BANK[MA][0:HALF, :].rearrange("p (k s) -> p k s", k=2)).then_inc(ont_ok, 1)

            def out_group(b, late):
                if not b.first and not late:
                    act.wait_ge(t1_ps, b.count(2))
                if late:
                    act.wait_ge(av_ps, b.count(3, 3))
                    nc.scalar.copy(OT[:, 2, :], BANK[O_BANK[1]][:, 0:S]).then_inc(ot_ok, 1)
                else:
                    act.wait_ge(av_ps, b.count(3, 2))
                    nc.scalar.copy(OT[:, 0:2, :], BANK[O_BANK[0]][:, :].rearrange("p (g s) -> p g s", g=2)).then_inc(ot_ok, 1)

            def exp(b, par, v):
                act.wait_ge(st_ps, b.count(SU, v + 1))
                if not b.first and v % 3 == 0:
                    act.wait_ge(av_ps, (b - 1).count(3, v // 3 + 1))
                nc.scalar.activation(PT[:, v, :], BANK[T_BANK[(SU * par + v) % 2]][:, :], ACT.Exp, scale=SCALE).then_inc(exp_ok, 1)

            def maxima(b, g):
                act.wait_ge(mt_ps, b.count(G, g + 1))
                bank = MA if g == 0 else MB
                nc.scalar.copy(MT[:, g, :], BANK[bank][0:2 * HG, 0:S // 2].bitcast(bf16)).then_inc(mt_ok, 1)

            def step(b, par, has_ahead, has_front, has_back, has_old):
                if has_front:
                    first_part(b + 1, 0)
                if has_back:
                    exp(b - 1, 1 - par, 6)
                    exp(b - 1, 1 - par, 7)
                    out_group(b - 1, False)
                if has_front:
                    middle(b + 1, 0)
                if has_back:
                    exp(b - 1, 1 - par, 8)
                maxima(b, 0)
                if has_front:
                    first_part(b + 1, 1)
                if has_front:
                    middle(b + 1, 1)
                if has_back:
                    out_group(b - 1, True)
                exp(b, par, 0)
                exp(b, par, 1)
                maxima(b, 1)
                exp(b, par, 2)
                if has_back:
                    outputs_t(b - 1)
                if has_ahead:
                    front(b + 2)
                exp(b, par, 3)
                maxima(b, 2)
                exp(b, par, 4)
                exp(b, par, 5)

            for t in range(TT):
                patches_t(t, 0)
                patches_t(t, 1)
                tokens(t, 0)
                tokens(t, 1)
                patches_t(t, 2)
                if t == 1:
                    deviations(2, SECOND)
                tokens(t, 2)
                tokens(t, 3)
                patches_t(t, 3)
                if t == 0:
                    for q in range(4, B // 2):
                        tokens(t, q)
                    deviations(1, EVEN)
            front(Image(0, 0))
            tokens(1, 4)
            act.wait_ge(ld_const, 16 * N_CONST)
            first_part(Image(0, 0), 0)
            tokens(1, 5)
            tokens(1, 6)
            middle(Image(0, 0), 0)
            first_part(Image(0, 0), 1)
            tokens(1, 7)
            middle(Image(0, 0), 1)
            front(Image(0, 1))
            deviations(3, ODD)
            step(Image(0, 0), 0, True, True, False, False)
            step(Image(0, 1), 1, True, True, True, False)
            with act.Fori(1, B // 2 - 1) as i:
                step(Image(i, 0), 0, True, True, True, True)
                step(Image(i, 1), 1, True, True, True, True)
            step(Image(0, B - 2), 0, False, True, True, True)
            step(Image(0, B - 1), 1, False, False, True, True)
            last = Image(0, B - 1)
            lim = NT - QD
            deviations(4, slice(0, lim))

            def tokens_t(k):
                act.wait_ge(x2t_ps, k + 1)
                if k >= 2:
                    act.wait_ge(lg_ps, k - 1)
                for c in range(2):
                    nc.scalar.copy(X2T[k % 2][:, c, :], BANK[pair(k) + c][0:HALF, :]).then_inc(x2t_ok, 1)

            def logits_t(k):
                act.wait_ge(lg_ps, k + 1)
                if k >= 1:
                    act.wait_ge(lt_ps, k)
                nc.scalar.copy(LGT[:, :], BANK[MB][:, 0:P]).then_inc(lgt_ok, 1)

            def gelu(u):
                act.wait_ge(lg_ok, u + 1)
                rows = slice(u * NH, (u + 1) * NH)
                nc.scalar.activation(GE[:, rows, :], LG[:, rows, 0:NODES], ACT.Gelu).then_inc(ge_ok, 1)

            def coefficient_parts(u):
                rows = slice(u * NH, (u + 1) * NH)
                act.wait_ge(co_ok, u + 1)
                nc.scalar.copy(C6[:, rows, 0:3 * NODES].rearrange("p t (a n) -> p t a n", a=3),
                               CO[:, rows, :].rearrange("p t (a n) -> p t a n", a=1).broadcast_to([P, NH, 3, NODES])).then_inc(ch_ok, 1)
                act.wait_ge(cr_ok, u + 1)
                nc.scalar.copy(C6[:, rows, 3 * NODES:5 * NODES].rearrange("p t (a n) -> p t a n", a=2),
                               CR[:, rows, :].rearrange("p t (a n) -> p t a n", a=1).broadcast_to([P, NH, 2, NODES])).then_inc(cm_ok, 1)

            def coefficients_t(k):
                act.wait_ge(cot_ps, k + 1)
                if k >= 2:
                    act.wait_ge(o_ps, 2 * (k - 1))
                nc.scalar.copy(COT[k % 2][:, :], BANK[k % 2][0:KO, 0:QD * P // 2].bitcast(bf16)).then_inc(cot_ok, 1)

            exp(last, 1, 6)
            exp(last, 1, 7)
            out_group(last, False)
            exp(last, 1, 8)
            tokens_t(0)
            out_group(last, True)
            logits_t(0)
            tokens_t(1)
            logits_t(1)
            tokens_t(2)
            outputs_t(last)
            logits_t(2)
            for k in range(3, NQ - 3):
                tokens_t(k)
                logits_t(k)
            deviations(5, slice(lim, NT))
            tokens_t(NQ - 3)
            tokens_t(NQ - 2)
            logits_t(NQ - 3)
            gelu(0)
            tokens_t(NQ - 1)
            logits_t(NQ - 2)
            logits_t(NQ - 1)
            coefficient_parts(0)
            gelu(1)
            coefficients_t(0)
            coefficients_t(1)
            coefficient_parts(1)
            for k in range(2, NQ):
                coefficients_t(k)

        @block.vector
        def _(dve):
            job = 0

            def d_bank():
                return BANK[4 + job % 4]

            def patches(t):
                dve.wait_ge(g0_in[t], 16 * GP)
                nc.vector.tensor_copy(G0R[:, t, :, :].rearrange("p b (g f) -> p g b f", f=F0),
                                      G0[:, t, :, :].rearrange("p g (b f) -> p g b f", f=F0)).then_inc(g0r_ok, 1)

            dve.wait_ge(g2_in, 32)
            for q in range(4):
                nc.vector.tensor_copy(G2R[:, 4 * q:4 * q + 4, :].rearrange("p b (g f) -> p g b f", g=2),
                                      G2[:, :, 4 * q * F2:4 * (q + 1) * F2].rearrange("p g (b f) -> p g b f", b=4)).then_inc(g2r_ok, 1)
            dve.wait_ge(g1_in, 16 * (GP // 2))
            nc.vector.tensor_copy(G1R[:, :, :].rearrange("p b (g f) -> p g b f", f=F1), G1[:, :, :].rearrange("p g (b f) -> p g b f", f=F1)).then_inc(g1r_ok, 1)
            for q in range(4):
                dve.wait_ge(pe_d, job + 1)
                nc.vector.tensor_copy(G1T[:, :, 4 * q:4 * q + 4, :],
                                      d_bank()[0:HALF, :].rearrange("p (b g t) -> p g b t", b=4, g=2)).then_inc(dve_d, 1)
                job += 1
            dve.wait_ge(ld_const, 16 * N_CONST)
            dve.wait_ge(pe_d, job + 1)
            nc.vector.tensor_tensor(CB[:, :], d_bank()[:, 0:D], BFB[:, :], ALU.add).then_inc(dve_d, 1)
            job += 1
            dve.wait_ge(pe_d, job + 1)
            nc.vector.tensor_copy(C0[:, :], d_bank()[0:GP * F0, 0:D]).then_inc(dve_d, 1)
            job += 1
            dve.wait_ge(dve_d, 6)
            for q in range(B // 2):
                dve.wait_ge(pe_d, job + 1)
                nc.vector.tensor_tensor(RH[T1:P, 2 * q:2 * q + 2, :], d_bank()[T1:P, 0:2 * D].rearrange("p (b d) -> p b d", b=2),
                                        CB[T1:P, :].rearrange("p (a d) -> p a d", a=1).broadcast_to([T1, 2, D]), ALU.add).then_inc(dve_d, 1)
                job += 1
            done = [0]

            def statistics(t, q):
                dve.wait_ge(ht_ok, B // 2 * t + q + 1)
                for b in (2 * q, 2 * q + 1):
                    nc.vector.bn_stats(ST[:, TT * b + t, :], HT[:, TT * b + t, :]).then_inc(stat, 1)
                    done[0] += 1

            def variances(tiles):
                nc.vector.tensor_scalar(VE[:, tiles], MV[:, tiles, 1], EPS, None, ALU.add).then_inc(var_ok, 1)

            def aggregate(tiles):
                dve.wait_ge(stat, done[0])
                for k in range(tiles.start, tiles.stop, tiles.step):
                    nc.vector.bn_aggr(MV[:, k, :], ST[:, k, :]).then_inc(stat, 1)
                    done[0] += 1
                dve.wait_ge(stat, done[0])
                variances(tiles)

            def rstd(round_, tiles):
                dve.wait_ge(sd_ok, round_)
                nc.vector.reciprocal(RSTD[:, tiles], SD[:, tiles]).then_inc(rstd_ok, 1)
                dve.wait_ge(rstd_ok, round_)
                nc.vector.scalar_tensor_tensor(NMR[:, tiles], MV[:, tiles, 0], -1.0, RSTD[:, tiles], ALU.mult, ALU.mult).then_inc(nmr_ok, 1)

            def norm(b):
                if not b.first:
                    dve.wait_ge(xt_ps, b.count(1))
                for t in range(TT):
                    k = b.count(TT, t)
                    ins = nc.vector.tensor_scalar(XN[:, t, :], HT[:, bass.ds(k, 1), :].rearrange("p a d -> p (a d)"),
                                                  RSTD[:, bass.ds(k, 1)], NMR[:, bass.ds(k, 1)], ALU.mult, ALU.add)
                ins.then_inc(xn_ok, 1)

            def row_max(b, par, u):
                dve.wait_ge(s_ps, b.count(SU, u + 1))
                if u % 3 == 0 and not b.first:
                    dve.wait_ge(mp_ok, (b - 1).count(G, u // 3 + 1))
                bank = BANK[S_BANK[(SU * par + u) % 2]]
                g, r = u // 3, u % 3
                if r == 0:
                    nc.vector.reduce_max(MX[:, 0, HG * g:HG * (g + 1)], bank[:, :].rearrange("p (h k) -> p h k", h=4), AX.X).then_inc(max_ok, 1)
                else:
                    nc.vector.reduce_max(MX[:, 1, HG * g + 2 * r - 2:HG * g + 2 * r], bank[:, :].rearrange("p (h k) -> p h k", h=2), AX.X).then_inc(max_ok, 1)

            def rest(b, w):
                dve.wait_ge(p0_ok, b.count(2, w + 1))
                if not b.first:
                    dve.wait_ge(p2_ok, (b - 1).count(2, w + 1))
                for m in range(2):
                    ins = nc.vector.scalar_tensor_tensor(RES[:, 2 * w + m, :], BANK[MB][0:HALF, m * S:(m + 1) * S],
                                                         BQK[:, 2 * w + m:2 * w + m + 1], PART[0][:, 2 * w + m, :], ALU.add, ALU.subtract)
                ins.then_inc(r_ok, 1)

            def values(b, par):
                dve.wait_ge(v_ps, b.count(1, 1))
                if not (b.first or b.second):
                    dve.wait_ge(av_ps, (b - 1).count(3))
                for t in range(TT):
                    ins = nc.vector.tensor_tensor(VA[par][:, t, :, 0:HS], BANK[MB][:, t * D:(t + 1) * D].rearrange("p (h d) -> p h d", h=H),
                                                  BV[:, :].rearrange("p (h d) -> p h d", h=H), ALU.add)
                ins.then_inc(v_ok, 1)

            def normalise(b, t):
                dve.wait_ge(t1_ps, b.count(2, t + 1))
                o = BANK[T1_BANK[t]][:, 0:3 * P].rearrange("p (h c) -> p h c", h=H)
                nc.vector.reciprocal(RC[:, t, :], o[:, :, HS]).then_inc(rc_ok, 1)
                dve.wait_ge(rc_ok, b.count(2, t + 1))
                nc.vector.tensor_tensor(ON[:, t, :].rearrange("p (h c) -> p h c", h=H), o[:, :, 0:HS],
                                        RC[:, t, :].rearrange("p (h a) -> p h a", a=1).broadcast_to([P, H, HS]), ALU.mult).then_inc(on_ok, 1)

            def minus_max(b, g):
                dve.wait_ge(max_ok, b.count(SU, 3 * g + 3))
                if not b.first:
                    dve.wait_ge(mt_ps, (b - 1).count(G, g + 1))
                mx = MX[:, :, HG * g:HG * (g + 1)]
                nc.vector.tensor_scalar(MP[:, g, :, 0, :], mx, -1.0, None, ALU.mult).then_inc(mh_ok, 1)
                dve.wait_ge(mh_ok, b.count(G, g + 1))
                nc.vector.scalar_tensor_tensor(MP[:, g, :, 1, :], mx, -1.0, MP[:, g, :, 0, :], ALU.mult, ALU.subtract).then_inc(mp_ok, 1)

            def residual(b):
                dve.wait_ge(pj_ps, b.count(1, 1))
                hv = HT[:, bass.ds(b.count(TT), TT), :]
                nc.vector.tensor_tensor(H2[:, :, :], BANK[MA][:, 0:2 * D].rearrange("p (t d) -> p t d", t=2), hv, ALU.add).then_inc(h2_ok, 1)

            def residual_bias(b):
                hv = HT[:, bass.ds(b.count(TT), TT), :]
                dve.wait_ge(h2_ok, b.count(2, 1))
                nc.vector.tensor_tensor(H2[:, :, :], H2[:, :, :], BP[:, :].rearrange("p (a d) -> p a d", a=1).broadcast_to([P, 2, D]),
                                        ALU.add).then_inc(h2_ok, 1)
                dve.wait_ge(h2_ok, b.count(2, 2))
                for t in range(TT):
                    nc.vector.bn_stats(ST2[:, t, :], H2[:, t, :]).then_inc(st2_ok, 1)
                dve.wait_ge(st2_ok, b.count(2, 2))
                nc.vector.tensor_scalar(hv, H2[:, :, :], 1.0, None, ALU.mult)
                for t in range(TT):
                    nc.vector.bn_aggr(MV2[:, t, :], ST2[:, t, :]).then_inc(mv2_ok, 1)
                dve.wait_ge(mv2_ok, b.count(2, 2))
                nc.vector.tensor_scalar(MV[:, bass.ds(b.count(TT), TT), :], MV2[:, :, :], 1.0, None, ALU.mult).then_inc(mvh_ok, 1)

            def step(b, par, has_ahead, has_front, has_back, has_old):
                if has_ahead:
                    norm(b + 2)
                row_max(b, par, 0)
                if has_front:
                    rest(b + 1, 0)
                row_max(b, par, 1)
                row_max(b, par, 2)
                minus_max(b, 0)
                row_max(b, par, 3)
                if has_front:
                    rest(b + 1, 1)
                row_max(b, par, 4)
                if has_old:
                    residual(b - 2)
                row_max(b, par, 5)
                minus_max(b, 1)
                if has_back:
                    normalise(b - 1, 0)
                    normalise(b - 1, 1)
                row_max(b, par, 6)
                row_max(b, par, 7)
                if has_front:
                    values(b + 1, 1 - par)
                row_max(b, par, 8)
                minus_max(b, 2)
                if has_old:
                    residual_bias(b - 2)

            patches(0)
            for q in range(B // 2):
                statistics(0, q)
            aggregate(EVEN)
            rstd(1, EVEN)
            patches(1)
            statistics(1, 0)
            aggregate(SECOND)
            statistics(1, 1)
            rstd(2, SECOND)
            dve.wait_ge(nmr_ok, 2)
            norm(Image(0, 0))
            for q in range(2, 5):
                statistics(1, q)
            rest(Image(0, 0), 0)
            statistics(1, 5)
            statistics(1, 6)
            rest(Image(0, 0), 1)
            statistics(1, 7)
            norm(Image(0, 1))
            dve.wait_ge(va_init, 6)
            values(Image(0, 0), 0)
            aggregate(ODD)
            rstd(3, ODD)
            dve.wait_ge(nmr_ok, 3)
            nc.vector.tensor_copy(WPART[:, 0, :], WEX).then_inc(w6_ok, 1)
            dve.wait_ge(w6_ok, 1)
            nc.vector.tensor_tensor(WR, WEX, WPART[:, 0, :], ALU.subtract).then_inc(w6_ok, 1)
            dve.wait_ge(w6_ok, 2)
            nc.vector.tensor_copy(WPART[:, 1, :], WR).then_inc(w6_ok, 1)
            dve.wait_ge(w6_ok, 3)
            nc.vector.tensor_tensor(WPART[:, 2, :], WR, WPART[:, 1, :], ALU.subtract).then_inc(w6_ok, 1)
            dve.wait_ge(w6_ok, 4)
            nc.vector.tensor_scalar(W6[:, :], WPART[:, 0, :], SEL[:, 0:1], None, ALU.mult).then_inc(w6_ok, 1)
            for n in range(1, PARTS):
                dve.wait_ge(w6_ok, 4 + n)
                nc.vector.scalar_tensor_tensor(W6[:, :], WPART[:, n, :], SEL[:, n:n + 1], W6[:, :], ALU.mult, ALU.add).then_inc(w6_ok, 1)
            step(Image(0, 0), 0, True, True, False, False)
            step(Image(0, 1), 1, True, True, True, False)
            with dve.Fori(1, B // 2 - 1) as i:
                step(Image(i, 0), 0, True, True, True, True)
                step(Image(i, 1), 1, True, True, True, True)
            step(Image(0, B - 2), 0, False, True, True, True)
            step(Image(0, B - 1), 1, False, False, True, True)
            dve.wait_ge(mvh_ok, B - 2)
            lim = NT - QD
            variances(slice(0, lim))
            rstd(4, slice(0, lim))

            def norm2(k):
                dve.wait_ge(nmr_ok, 4 if k < NQ - 1 else 5)
                if k >= XQ:
                    dve.wait_ge(x2t_ps, k - XQ + 1)
                for j in range(QD * k, QD * k + (2 if k >= 2 else 4)):
                    ins = nc.vector.tensor_scalar(X2[:, j % (XQ * QD), :], HT[:, j, :], RSTD[:, j:j + 1], NMR[:, j:j + 1], ALU.mult, ALU.add)
                ins.then_inc(x2_ok, 1)

            links = [0]

            def link(ins):
                links[0] += 1
                ins.then_inc(tree, 1)
                dve.wait_ge(tree, links[0])

            def copy_logits(u):
                rows = slice(u * NH, (u + 1) * NH)
                dve.wait_ge(lt_ps, (u + 1) * NQ // 2)
                nc.vector.tensor_copy(LG[:, rows, :], BANK[O_BANK[u]][:, :].rearrange("p (t n) -> p t n", t=NH)).then_inc(lg_ok, 1)

            def walk(u):
                rows = slice(u * NH, (u + 1) * NH)
                dve.wait_ge(lg_ok, u + 1)
                nc.vector.tensor_scalar(SG[:, rows, :], LG[:, rows, 0:NODES], 0.0, None, ALU.is_gt).then_inc(tree, 1)
                nc.vector.tensor_scalar(NS[:, rows, :], LG[:, rows, 0:NODES], 0.0, None, ALU.is_le).then_inc(tree, 1)
                links[0] += 2
                link(nc.vector.memset(RE[:, rows, 0:1], 1.0))
                for lo, hi in ((0, 1), (1, 3), (3, 7), (7, 10)):
                    kids = RE[:, rows, 2 * lo + 1:2 * hi + 1].rearrange("p t (n c) -> p t n c", c=2)
                    nc.vector.tensor_tensor(kids[:, :, :, 0], RE[:, rows, lo:hi], NS[:, rows, lo:hi], ALU.mult).then_inc(tree, 1)
                    links[0] += 1
                    link(nc.vector.tensor_tensor(kids[:, :, :, 1], RE[:, rows, lo:hi], SG[:, rows, lo:hi], ALU.mult))
                link(nc.vector.reduce_sum(RE[:, rows, 21:22].rearrange("p t a -> p (t a)"), RE[:, rows, 15:20], AX.X))
                link(nc.vector.tensor_scalar(RE[:, rows, 20:21], RE[:, rows, 21:22], -1.0, 6.0, ALU.mult, ALU.add))

            def coefficients(u):
                rows = slice(u * NH, (u + 1) * NH)
                dve.wait_ge(ge_ok, u + 1)
                nc.vector.tensor_tensor(QE[:, rows, 0:11], RE[:, rows, 10:21], GE[:, rows, 10:21], ALU.mult).then_inc(tree, 1)
                nc.vector.memset(CO[:, rows, 0:1], 0.0).then_inc(tree, 1)
                links[0] += 2
                link(nc.vector.tensor_tensor(QQ[:, rows, :], RE[:, rows, 0:10], GE[:, rows, 0:10], ALU.mult))
                nc.vector.tensor_tensor(QE[:, rows, 11:12], QQ[:, rows, 9:10], SG[:, rows, 9:10], ALU.mult).then_inc(tree, 1)
                kids = CO[:, rows, 1:21].rearrange("p t (n c) -> p t n c", c=2)
                nc.vector.tensor_tensor(kids[:, :, :, 0], QQ[:, rows, :], NS[:, rows, 0:10], ALU.mult).then_inc(tree, 1)
                links[0] += 2
                link(nc.vector.tensor_tensor(kids[:, :, 0:9, 1], QQ[:, rows, 0:9], SG[:, rows, 0:9], ALU.mult))
                nc.vector.reduce_sum(CO[:, rows, 20:21].rearrange("p t a -> p (t a)"), QE[:, rows, :], AX.X).then_inc(co_ok, 1)

            def output(k):
                for j in range(2 * k, 2 * k + 2):
                    dve.wait_ge(o_ps, j + 1)
                    h = HT[:, 2 * j:2 * j + 2, :].rearrange("p t d -> p (t d)")
                    nc.vector.tensor_tensor(h, BANK[OUT_BANK[j % 4]][:, 0:2 * D], h, ALU.add).then_inc(o_ok, 1)

            for k in range(XQ):
                norm2(k)
            residual(Image(0, B - 2))
            residual_bias(Image(0, B - 2))
            norm2(4)
            normalise(Image(0, B - 1), 0)
            normalise(Image(0, B - 1), 1)
            norm2(5)
            norm2(6)
            residual(Image(0, B - 1))
            residual_bias(Image(0, B - 1))
            dve.wait_ge(mvh_ok, B)
            variances(slice(lim, NT))
            copy_logits(0)
            rstd(5, slice(lim, NT))
            norm2(7)
            walk(0)
            coefficients(0)
            copy_logits(1)
            walk(1)
            coefficients(1)
            output(0)
            dve.wait_ge(ch_ok, 2)
            nc.vector.tensor_tensor(CR[:, NH:, :], CO[:, NH:, :], C6[:, NH:, 0:NODES], ALU.subtract).then_inc(cr_ok, 1)
            output(1)
            dve.wait_ge(cm_ok, 2)
            nc.vector.tensor_tensor(C6[:, NH:, 5 * NODES:], CR[:, NH:, :], C6[:, NH:, 3 * NODES:4 * NODES], ALU.subtract).then_inc(c6_ok, 1)
            for k in range(2, NQ):
                output(k)

        @block.tensor
        def _(pe):
            pe.wait_ge(ld_first, 16 * N_FIRST)
            ja, jd = 0, 0

            def a_bank():
                if ja >= 4:
                    pe.wait_ge(act_a, ja - 3 + (1 if ja >= 10 else 0))
                return BANK[ja % 4]

            def d_bank():
                if jd >= 4:
                    pe.wait_ge(dve_d, jd - 3)
                return BANK[4 + jd % 4]

            pe.wait_ge(g2_in, 32)
            for q in range(4):
                bank = a_bank()
                pe.wait_ge(g2r_ok, q + 1)
                for j in range(4):
                    ins = nc.tensor.transpose(bank[0:2 * F2, j * P:(j + 1) * P], G2R[:, 4 * q + j, :], ID[:, :])
                ins.then_inc(pe_a, 1)
                ja += 1
            bank = a_bank()
            pe.wait_ge(act_a, 4)
            for g in range(GP // 2):
                ins = nc.tensor.matmul(bank[0:EMB, 0:B * T2], W2S[:, g, :], G2T[:, g, :, :].rearrange("f b t -> f (b t)"), start=g == 0, stop=g == GP // 2 - 1)
            ins.then_inc(pe_a, 1)
            ja += 1
            pe.wait_ge(g1r_ok, 1)
            for q in range(4):
                bank = d_bank()
                for j in range(4):
                    ins = nc.tensor.transpose(bank[0:HALF, j * P:(j + 1) * P],
                                              G1R[:, 4 * q + j, :], ID[:, :])
                ins.then_inc(pe_d, 1)
                jd += 1
            bank = a_bank()
            pe.wait_ge(act_a, 5)
            for g in range(2):
                ins = nc.tensor.matmul(bank[:, g * D:(g + 1) * D], E2[:, g * P:(g + 1) * P], WFS[:, 2, :], start=True, stop=True)
            ins.then_inc(pe_a, 1)
            ja += 1
            nc.tensor.matmul(d_bank()[:, 0:D], BC[:, 0:1].broadcast_to([EMB, P]), WFS[:, 0, :], start=True, stop=True).then_inc(pe_d, 1)
            jd += 1
            nc.tensor.matmul(d_bank()[0:GP * F0, 0:D], W0S[:, :], WFS[:, 0, :], start=True, stop=True).then_inc(pe_d, 1)
            jd += 1
            pe.wait_ge(dve_d, 4)
            for c in range(2):
                bank = a_bank()
                for g in range(2):
                    ins = nc.tensor.matmul(bank[0:EMB, :], W1S[:, g, :], G1T[:, g, 8 * c:8 * c + 8, :].rearrange("f b t -> f (b t)"),
                                           start=g == 0, stop=g == 1)
                ins.then_inc(pe_a, 1)
                ja += 1
            def patches_t(t, q):
                n = ja + 4 * t + q
                if q == 0:
                    pe.wait_ge(g0r_ok, t + 1)
                pe.wait_ge(act_a, n - 3 + (1 if n >= 10 else 0))
                for j in range(4):
                    ins = nc.tensor.transpose(BANK[n % 4][0:GP * F0, j * P:(j + 1) * P], G0R[:, t, 4 * q + j, :], ID[:, :])
                ins.then_inc(pe_a, 1)

            pe.wait_ge(act_a, 9)
            for q in range(B // 2):
                bank = d_bank()
                for j in range(2):
                    b = 2 * q + j
                    ins = nc.tensor.matmul(bank[T1:P, j * D:(j + 1) * D], E1[:, b * T1:(b + 1) * T1], WFS[:, 1, :], start=True, stop=True)
                ins.then_inc(pe_d, 1)
                jd += 1

            def tokens(t, q):
                n = B // 2 * t + q
                if n == 0:
                    pe.wait_ge(ld_z2, 16 * B)
                    pe.wait_ge(ld_interp, 16)
                if n < 3:
                    pe.wait_ge(dve_d, 14)
                else:
                    pe.wait_ge(ht_ok, n - 2)
                pe.wait_ge(act_a, 9 + 4 * t + q // 2 + 1)
                for j in range(2):
                    b = 2 * q + j
                    ins = nc.tensor.matmul(BANK[H_BANK[n % 3]][:, j * D:(j + 1) * D], LH[:, TT * b + t, :], RH[:, b, :], start=True, stop=True)
                ins.then_inc(ht_ps, 1)

            def xn_t(b):
                pe.wait_ge(xn_ok, b.count(1, 1))
                if b.second:
                    pe.wait_ge(v_ok, 1)
                elif not b.first:
                    pe.wait_ge(v_ok, (b - 1).count(1, 1))
                for k in range(2):
                    for t in range(TT):
                        ins = nc.tensor.transpose(BANK[MB][0:HALF, k * S + t * P:k * S + (t + 1) * P], XN[:, t, k * HALF:(k + 1) * HALF], ID[:, :])
                ins.then_inc(xt_ps, 1)

            def qk(b, w):
                pe.wait_ge(xnt_ok, b.count(1, 1))
                if w == 0 and not (b.first or b.second):
                    pe.wait_ge(mt_ok, (b - 2).count(G, G))
                if w == 1:
                    pe.wait_ge(r_ok, b.count(2, 1))
                for m in range(2):
                    for k in range(2):
                        ins = nc.tensor.matmul(BANK[MB][0:HALF, m * S:(m + 1) * S], WA[:, k, (2 * w + m) * HALF:(2 * w + m + 1) * HALF],
                                               XNT[:, k, :], start=k == 0, stop=k == 1)
                ins.then_inc(qk_ps, 1)

            def v_proj(b):
                if b.first:
                    pe.wait_ge(r_ok, 2)
                else:
                    pe.wait_ge(mt_ok, (b - 1).count(G, 2))
                for t in range(TT):
                    for k in range(2):
                        ins = nc.tensor.matmul(BANK[MB][:, t * D:(t + 1) * D], XNT[:, k, t * P:(t + 1) * P], WA[:, k, 2 * D:3 * D],
                                               start=k == 0, stop=k == 1)
                ins.then_inc(v_ps, 1)

            def scores(b, par, u):
                n = SU * par + u
                if b.first:
                    if u >= 2:
                        pe.wait_ge(max_ok, u - 1)
                else:
                    pe.wait_ge(max_ok, b.count(SU, u - 1))
                bank = BANK[S_BANK[n % 2]]
                g, r = u // 3, u % 3
                if r == 0:
                    for j in range(HG):
                        h = HG * g + j
                        nc.tensor.matmul(bank[:, j * P:(j + 1) * P], QS[par][0:KQ, h, 0:P], KS[par][0:KQ, h, 0:P], start=j == 0, stop=False)
                    nc.tensor.matmul(bank[:, :], IDB[:, :], MASKQ[:, :, :].rearrange("p a k -> p (a k)"), start=False, stop=True).then_inc(s_ps, 1)
                else:
                    for j in range(2):
                        h = HG * g + 2 * (r - 1) + j
                        nc.tensor.matmul(bank[:, j * S:(j + 1) * S], QS[par][0:KQ, h, P:S], KS[par][0:KQ, h, :], start=j == 0, stop=False)
                    nc.tensor.matmul(bank[:, :].rearrange("p (h k) -> p h k", h=2)[:, :, P:S], IDB[:, :], MASKQ[:, 0:2, :],
                                     start=False, stop=True).then_inc(s_ps, 1)

            def max_t(b, g, has_ahead=False):
                pe.wait_ge(mp_ok, b.count(G, g + 1))
                bank = MA if g == 0 else MB
                if g == 0 and not (b.first or b.second):
                    pe.wait_ge(ont_ok, (b - 1).count(1))
                if g == 1 and not b.last:
                    pe.wait_ge(r_ok, b.count(2, 4))
                if g == 2 and not b.last:
                    if has_ahead:
                        pe.wait_ge(xnt_ok, b.count(1, 3))
                    else:
                        pe.wait_ge(v_ok, b.count(1, 2))
                if g > 0 and b.last:
                    pe.wait_ge(mt_ok, b.count(G, 0 if g == 1 else 2))
                for t in range(TT):
                    ins = nc.tensor.transpose(BANK[bank][0:2 * HG, t * P // 2:(t + 1) * P // 2].bitcast(bf16),
                                              MP[:, g, t, :, :].rearrange("p a h -> p (a h)"), IDB[:, :])
                ins.then_inc(mt_ps, 1)

            def scores_t(b, par, v):
                if b.first:
                    if v >= 2:
                        pe.wait_ge(exp_ok, v - 1)
                else:
                    pe.wait_ge(exp_ok, b.count(SU, v - 1))
                bank = BANK[T_BANK[(SU * par + v) % 2]]
                g, r = v // 3, v % 3
                if r == 0:
                    pe.wait_ge(m_in, b.count(G * 16, 16 * (g + 1)))
                if r < 2:
                    for j in range(2):
                        h = HG * g + 2 * r + j
                        ins = nc.tensor.matmul(bank[:, j * S:(j + 1) * S], KS[par][:, h, 0:P], QS[par][:, h, :], start=j == 0, stop=j == 1)
                else:
                    for j in range(HG):
                        h = HG * g + j
                        ins = nc.tensor.matmul(bank[:, j * P:(j + 1) * P], KS[par][:, h, P:S], QS[par][:, h, P:S], start=j == 0, stop=j == HG - 1)
                ins.then_inc(st_ps, 1)

            def weighted(b, par, g):
                pe.wait_ge(cut_ok, b.count(SU, 3 * g + 3))
                if g == 0 and not b.first:
                    pe.wait_ge(ot_ok, (b - 1).count(2, 1))
                if g == 2 and not b.first:
                    pe.wait_ge(on_ok, b.count(2))
                if g == 0:
                    pe.wait_ge(v_ok, b.count(1, 1))
                bank = BANK[O_BANK[g // 2]]
                c = (g % 2) * S
                for j in range(4):
                    nc.tensor.matmul(bank[32 * j:32 * j + 32, c:c + S], VA[par][:, 0, 4 * g + j, :],
                                     PT[:, 3 * g + j // 2, (j % 2) * S:(j % 2 + 1) * S], start=True, stop=False, skip_group_check=True)
                for j in range(4):
                    ins = nc.tensor.matmul(bank[32 * j:32 * j + 32, c + P:c + S], VA[par][:, 1, 4 * g + j, :],
                                           PT[:, 3 * g + 2, j * P:(j + 1) * P], start=False, stop=True, skip_group_check=True)
                ins.then_inc(av_ps, 1)

            def out_t(b, t):
                pe.wait_ge(ot_ok, b.count(2, 2))
                if t == 1:
                    pass
                elif b.first:
                    pe.wait_ge(mt_ok, b.count(G, G + 1))
                else:
                    pe.wait_ge(h2_ok, (b - 1).count(2, 1))
                for g in range(3):
                    ins = nc.tensor.transpose(BANK[T1_BANK[t]][:, g * P:(g + 1) * P], OT[:, g, t * P:(t + 1) * P], ID[:, :])
                ins.then_inc(t1_ps, 1)

            def on_t(b):
                pe.wait_ge(on_ok, b.count(2, 2))
                for k in range(2):
                    for t in range(TT):
                        ins = nc.tensor.transpose(BANK[MA][0:HALF, k * S + t * P:k * S + (t + 1) * P], ON[:, t, k * HALF:(k + 1) * HALF], ID[:, :])
                ins.then_inc(t2_ps, 1)

            def project(b):
                pe.wait_ge(ont_ok, b.count(1, 1))
                if not b.last and not b.late:
                    pe.wait_ge(mt_ok, b.count(G, 2 * G + 1))
                for t in range(TT):
                    for k in range(2):
                        ins = nc.tensor.matmul(BANK[MA][:, t * D:(t + 1) * D], ONT[:, k, t * P:(t + 1) * P], WP[:, k, :], start=k == 0, stop=k == 1)
                ins.then_inc(pj_ps, 1)

            def step(b, par, has_ahead, has_front, has_back, has_old):
                if has_front:
                    qk(b + 1, 0)
                pe.wait_ge(stacked, b.count(6 * 16, 6 * 16))
                scores(b, par, 0)
                scores(b, par, 1)
                if has_back:
                    scores_t(b - 1, 1 - par, 6)
                    scores_t(b - 1, 1 - par, 7)
                    weighted(b - 1, 1 - par, 1)
                scores(b, par, 2)
                if has_back:
                    scores_t(b - 1, 1 - par, 8)
                if has_front:
                    qk(b + 1, 1)
                max_t(b, 0)
                scores(b, par, 3)
                scores(b, par, 4)
                if has_old:
                    project(b - 2)
                if has_back:
                    weighted(b - 1, 1 - par, 2)
                scores(b, par, 5)
                scores_t(b, par, 0)
                scores_t(b, par, 1)
                scores(b, par, 6)
                if has_back:
                    out_t(b - 1, 0)
                    out_t(b - 1, 1)
                max_t(b, 1)
                scores_t(b, par, 2)
                scores(b, par, 7)
                if has_front:
                    v_proj(b + 1)
                if has_back:
                    on_t(b - 1)
                scores(b, par, 8)
                if has_ahead:
                    xn_t(b + 2)
                scores_t(b, par, 3)
                scores_t(b, par, 4)
                max_t(b, 2, has_ahead)
                weighted(b, par, 0)
                scores_t(b, par, 5)

            for t in range(TT):
                patches_t(t, 0)
                patches_t(t, 1)
                tokens(t, 0)
                tokens(t, 1)
                patches_t(t, 2)
                tokens(t, 2)
                tokens(t, 3)
                patches_t(t, 3)
                if t == 0:
                    for q in range(4, B // 2):
                        tokens(t, q)
            xn_t(Image(0, 0))
            tokens(1, 4)
            pe.wait_ge(ld_const, 16 * N_CONST)
            qk(Image(0, 0), 0)
            tokens(1, 5)
            tokens(1, 6)
            qk(Image(0, 0), 1)
            tokens(1, 7)
            v_proj(Image(0, 0))
            xn_t(Image(0, 1))
            pe.wait_ge(act_a, 17)
            pe.wait_ge(ht_ok, B)
            step(Image(0, 0), 0, True, True, False, False)
            step(Image(0, 1), 1, True, True, True, False)
            with pe.Fori(1, B // 2 - 1) as i:
                step(Image(i, 0), 0, True, True, True, True)
                step(Image(i, 1), 1, True, True, True, True)
            step(Image(0, B - 2), 0, False, True, True, True)
            step(Image(0, B - 1), 1, False, False, True, True)
            last = Image(0, B - 1)
            def tokens_t(k):
                pe.wait_ge(x2_ok, k + 1)
                if k >= 2:
                    pe.wait_ge(x2p_ok, k - 1)
                if k == 0:
                    pe.wait_ge(max_ok, SU * B)
                elif k == 2:
                    pe.wait_ge(exp_ok, SU * B)
                else:
                    pe.wait_ge(x2t_ok, 2 * max(k - 1, 1))
                for c in range(2):
                    for j in range(QD):
                        ins = nc.tensor.transpose(BANK[pair(k) + c][0:HALF, j * P:(j + 1) * P],
                                                  X2[:, (QD * k + j) % (XQ * QD), c * HALF:(c + 1) * HALF], ID[:, :])
                ins.then_inc(x2t_ps, 1)

            def logits(k):
                pe.wait_ge(x2t_ok, 2 * (k + 1))
                if k == 0:
                    pe.wait_ge(mt_ok, G * B)
                else:
                    pe.wait_ge(lgt_ok, k)
                for c in range(2):
                    for j in range(QD):
                        ins = nc.tensor.matmul(BANK[MB][NP * j:NP * (j + 1), 0:P], WIN[:, c, :], X2T[k % 2][:, c, j * P:(j + 1) * P],
                                               start=c == 0, stop=c == 1, skip_group_check=True)
                ins.then_inc(lg_ps, 1)

            def logits_back(k):
                pe.wait_ge(lgt_ok, k + 1)
                u = k // (NQ // 2)
                if k % (NQ // 2) == 0:
                    if u == 0:
                        pe.wait_ge(ot_ok, 2 * B - 1)
                    else:
                        pe.wait_ge(on_ok, 2 * B)
                c = k % (NQ // 2) * P
                nc.tensor.transpose(BANK[O_BANK[u]][:, c:c + P], LGT[:, :], ID[:, :]).then_inc(lt_ps, 1)

            scores_t(last, 1, 6)
            scores_t(last, 1, 7)
            weighted(last, 1, 1)
            scores_t(last, 1, 8)
            tokens_t(0)
            project(Image(0, B - 2))
            weighted(last, 1, 2)
            logits(0)
            tokens_t(1)
            out_t(last, 0)
            out_t(last, 1)
            logits(1)
            logits_back(0)
            tokens_t(2)
            on_t(last)
            logits(2)
            logits_back(1)
            tokens_t(3)
            project(last)
            for k in range(3, NQ - 1):
                tokens_t(k + 1)
                logits(k)
                logits_back(k - 1)
            logits_back(NQ - 2)
            logits(NQ - 1)
            logits_back(NQ - 1)

            def coefficients_t(k):
                pe.wait_ge(c6_ok, k // (NQ // 2) + 1)
                if k == 0:
                    pe.wait_ge(x2t_ok, 2 * NQ)
                elif k >= 2:
                    pe.wait_ge(cot_ok, k - 1)
                for j in range(QD):
                    ins = nc.tensor.transpose(BANK[k % 2][0:KO, j * P // 2:(j + 1) * P // 2].bitcast(bf16), C6[:, QD * k + j, :], IDB[:, :])
                ins.then_inc(cot_ps, 1)

            def output(k):
                pe.wait_ge(cot_ok, k + 1)
                for i in range(2):
                    j = 2 * k + i
                    if j == 2:
                        pe.wait_ge(h2_ok, 2 * B)
                    elif j == 3:
                        pe.wait_ge(lgt_ok, NQ)
                    elif j >= 4:
                        pe.wait_ge(o_ok, j - 3)
                    for t in range(2):
                        ins = nc.tensor.matmul(BANK[OUT_BANK[j % 4]][:, t * D:(t + 1) * D],
                                               COT[k % 2][:, (2 * i + t) * P:(2 * i + t + 1) * P], W6[:, :], start=True, stop=True)
                    ins.then_inc(o_ps, 1)

            pe.wait_ge(w6_ok, 4 + PARTS)
            for k in range(NQ):
                coefficients_t(k)
                if k:
                    output(k - 1)
            output(NQ - 1)


def _interp(length):
    import numpy as np
    pos = np.clip((np.arange(S, dtype=np.float32) + np.float32(0.5)) * np.float32(length / S) - np.float32(0.5), 0, length - 1)
    lo = np.floor(pos).astype(np.int32)
    hi = np.minimum(lo + 1, length - 1)
    w = (pos - lo).astype(np.float32)
    m = np.zeros((length, S), np.float32)
    np.add.at(m, (lo, np.arange(S)), np.float32(1) - w)
    np.add.at(m, (hi, np.arange(S)), w)
    return m


def kernel(x, L0_tok_W0, L0_tok_b0, L0_tok_W1, L0_tok_b1, L0_tok_W2, L0_tok_b2, L0_tok_Wf, L0_tok_bf,
           L0_tok_idx0, L0_tok_idx1, L0_tok_idx2, L0_attn_W_attn, L0_attn_b_attn, L0_attn_W_proj, L0_attn_b_proj,
           L0_ffn_weights_in, L0_ffn_weights_out):
    import numpy as np
    import concourse.bacc as bacc
    from concourse.bass_utils import run_bass_kernel_spmd

    x = np.asarray(x)

    def patches(p):
        h = IMG // p
        t = x.reshape(B, CH, h, p, h, p).transpose(2, 4, 0, 3, 5, 1)
        return t.reshape(h * h, B * p * p * CH)

    def by_width(a):
        return a.reshape(a.shape[:-1] + (2, H, HS)).swapaxes(-1, -2).reshape(a.shape)

    w_attn, b_attn = np.asarray(L0_attn_W_attn), np.asarray(L0_attn_b_attn)
    i0, i1, i2 = (np.asarray(i) for i in (L0_tok_idx0, L0_tok_idx1, L0_tok_idx2))
    win = np.asarray(L0_ffn_weights_in)
    wout = np.asarray(L0_ffn_weights_out)
    bf16 = mybir.dt.np(mybir.dt.bfloat16)
    tri = np.tril(np.ones((P, P), bool))
    masked = np.float32(-2.0 ** 126)
    arrays = {
        "x0": patches(1), "x1": patches(2), "x2": patches(4),
        "ix0": i0.reshape(TT, P, GP).transpose(1, 0, 2).reshape(P, TT * GP),
        "ix1": i1.reshape(T1, 2, GP // 2).transpose(1, 0, 2).reshape(P, GP // 2),
        "ix2": i2.reshape(T2, 2, GP // 2).transpose(2, 0, 1).reshape(P, 2),
        "w0": np.asarray(L0_tok_W0), "w1t": np.asarray(L0_tok_W1).T, "w2t": np.asarray(L0_tok_W2).T,
        "wft": np.asarray(L0_tok_Wf).T, "bcol": np.stack([np.asarray(v) for v in (L0_tok_b0, L0_tok_b1, L0_tok_b2)], 1),
        "bf": np.asarray(L0_tok_bf),
        "wa": np.concatenate([by_width(w_attn[:, :2 * D]), w_attn[:, 2 * D:]], 1), "bqk": by_width(b_attn[:2 * D]).reshape(4, HALF).T,
        "bv": b_attn[2 * D:],
        "wp": np.asarray(L0_attn_W_proj), "bp": np.asarray(L0_attn_b_proj),
        "wint": np.concatenate([win, np.zeros((NP - NODES, D), np.float32)]).T,
        "wext": np.concatenate([wout] * 6),
        "sel": np.repeat(np.eye(PARTS, dtype=np.float32)[[0, 1, 2, 0, 1, 0]], NODES, 0),
        "identf": np.eye(P, dtype=np.float32), "identb": np.eye(P, dtype=np.float32).astype(bf16),
        "maskq": np.where(tri, np.float32(0), masked).astype(bf16),
        "interp": np.concatenate([_interp(T2), _interp(T1)]),
    }
    arrays = {n: np.ascontiguousarray(a) for n, a in arrays.items()}
    nc = bacc.Bacc("TRN2", target_bir_lowering=False, num_devices=1)
    args = [nc.dram_tensor(n, a.shape, mybir.dt.from_np(a.dtype), kind="ExternalInput").ap() for n, a in arrays.items()]
    out = nc.dram_tensor("out", (B * S, D), mybir.dt.float32, kind="ExternalOutput").ap()
    parts = nc.dram_tensor("parts", (B, PARTS, 4, HALF, S), mybir.dt.bfloat16, kind="Internal").ap()
    vit_tower_kernel(nc, *args, out, parts)
    r = run_bass_kernel_spmd(nc, [arrays], core_ids=[0])
    return r.results[0]["out"].reshape(B, S, D)
```
